# Optimizing a Trainium2 kernel written in Bass

```python
import numpy as np
import jax
import jax.numpy as jnp

def _softmax(x, axis=-1):
    return jax.nn.softmax(x, axis=axis)

def _gelu(x):
    return jax.nn.gelu(x, approximate=True)

def _silu(x):
    return jax.nn.silu(x)

def _sigmoid(x):
    return jax.nn.sigmoid(x)

def _layernorm(x, axis=-1, eps=1e-05):
    m = jnp.mean(x, axis=axis, keepdims=True)
    v = jnp.var(x, axis=axis, keepdims=True)
    return (x - m) / jnp.sqrt(v + eps)

def _scatter_add(tgt, idx, src, axis=0):
    return tgt.at[idx].add(src)

def _segment_sum(src, seg, n):
    return jax.ops.segment_sum(src, seg, n)
kernel_name = 'mk_gnn_preln_d2_gnn_r8_21c1cc'

def setup_inputs(seed: int=0):
    np.random.seed(seed)
    _w = jnp.asarray

    def _rec_inputs():
        import jax
        import jax.numpy as jnp
        _gk = jax.random.key(seed)
        x = -6.415e-05 + 1 * jax.random.normal(jax.random.fold_in(_gk, 1), (1250, 512), jnp.float32)
        src = jax.random.randint(jax.random.fold_in(_gk, 2), (20000,), 0, 1250, jnp.int32)
        dst = jnp.minimum((1250 * jax.random.uniform(jax.random.fold_in(_gk, 3), (20000,)) ** 2.0).astype(jnp.int32), 9999)
        _o = jnp.argsort(dst, stable=True)
        src = src[_o]
        dst = dst[_o]
        edge_type_2 = jax.random.randint(jax.random.fold_in(_gk, 13), (20000,), 0, 2, jnp.int32)
        edge_type_32 = jax.random.randint(jax.random.fold_in(_gk, 14), (20000,), 0, 32, jnp.int32)
        edge_weight1 = jax.random.uniform(jax.random.fold_in(_gk, 15), (20000, 1), jnp.float32, 0.0, 0.999996)
        return (x, src, dst, edge_type_2, edge_type_32, edge_weight1)
    x, src, dst, edge_type_2, edge_type_32, edge_weight1 = _rec_inputs()

    def _L0_gnn_setup():
        import jax, jax.numpy as jnp
        import numpy as np
        N_NODES = 2500
        N_EDGES = 40000
        IN_FEAT = 512
        OUT_FEAT = 512
        NUM_RELS = 32
        NUM_BASES = 8
        key = jax.random.key(seed)
        ks = jax.random.split(key, 8)
        x = jax.random.normal(ks[0], (N_NODES, IN_FEAT), dtype=jnp.float32)
        bases = jax.random.normal(ks[1], (NUM_BASES, IN_FEAT, OUT_FEAT), dtype=jnp.float32) * (1.0 / np.sqrt(IN_FEAT))
        w_comp = jax.random.normal(ks[2], (NUM_RELS, NUM_BASES), dtype=jnp.float32) * (1.0 / np.sqrt(NUM_BASES))
        h_bias = jnp.zeros((OUT_FEAT,), dtype=jnp.float32)
        norm = jax.random.uniform(ks[3], (N_EDGES, 1), dtype=jnp.float32)
        src = jax.random.randint(ks[4], (N_EDGES,), 0, N_NODES, dtype=jnp.int32)
        dst = jax.random.randint(ks[5], (N_EDGES,), 0, N_NODES, dtype=jnp.int32)
        etype = jnp.sort(jax.random.randint(ks[6], (N_EDGES,), 0, NUM_RELS, dtype=jnp.int32))
        return {'x': x, 'bases': bases, 'w_comp': w_comp, 'h_bias': h_bias, 'norm': norm, 'src': src, 'dst': dst, 'etype': etype}
    _L0_gnn_all = _L0_gnn_setup()
    _L0_gnn_in = {k: v for k, v in _L0_gnn_all.items() if k in ('bases', 'w_comp', 'h_bias')}
    del _L0_gnn_all

    def _L1_gnn_setup():
        import jax, jax.numpy as jnp
        import numpy as np
        NUM_RELATIONS = 2
        NUM_BASES = 30
        HIDDEN = 512
        N_NODES = 1250
        N_EDGES = 20000

        def rgcn_gate_layer(x, row, col, edge_type, basis, att, gate_w, root, bias):
            H = x.shape[1]
            w = jnp.einsum('rb,bio->rio', att, basis)
            x_j = x[col]
            msgs = []
            for r in range(NUM_RELATIONS):
                gate = jax.nn.sigmoid(x_j @ gate_w[r, :, 0])
                msgs.append(gate[:, None] * x_j @ w[r])
            msg = jnp.where((edge_type == 0)[:, None], msgs[0], msgs[1])
            agg = jax.ops.segment_sum(msg, row, num_segments=x.shape[0])
            return agg + x @ root + bias
        key = jax.random.key(seed)
        ks = jax.random.split(key, 16)
        H, R, B = (HIDDEN, NUM_RELATIONS, NUM_BASES)
        bound = 1.0 / np.sqrt(B * H)
        u = lambda k, shape: jax.random.uniform(k, shape, jnp.float32, -bound, bound)
        inp = {'x': jax.random.normal(ks[0], (N_NODES, H), jnp.float32), 'edge_index': jax.random.randint(ks[1], (2, N_EDGES), 0, N_NODES, jnp.int32), 'edge_type': jax.random.randint(ks[2], (N_EDGES,), 0, R, jnp.int32), 'basis1': u(ks[3], (B, H, H)), 'att1': u(ks[4], (R, B)), 'gate_w1': u(ks[5], (R, H, 1)), 'root1': u(ks[6], (H, H)), 'bias1': u(ks[7], (H,)), 'basis2': u(ks[8], (B, H, H)), 'att2': u(ks[9], (R, B)), 'gate_w2': u(ks[10], (R, H, 1)), 'root2': u(ks[11], (H, H)), 'bias2': u(ks[12], (H,))}
        return inp
    _L1_gnn_all = _L1_gnn_setup()
    _L1_gnn_in = {k: v for k, v in _L1_gnn_all.items() if k in ('basis1', 'att1', 'gate_w1', 'root1', 'bias1', 'basis2', 'att2', 'gate_w2', 'root2', 'bias2')}
    del _L1_gnn_all
    return {'x': x, 'src': src, 'dst': dst, 'edge_type_2': edge_type_2, 'edge_type_32': edge_type_32, 'edge_weight1': edge_weight1, 'L0_gnn_bases': _L0_gnn_in['bases'], 'L0_gnn_w_comp': _L0_gnn_in['w_comp'], 'L0_gnn_h_bias': _L0_gnn_in['h_bias'], 'L1_gnn_basis1': _L1_gnn_in['basis1'], 'L1_gnn_att1': _L1_gnn_in['att1'], 'L1_gnn_gate_w1': _L1_gnn_in['gate_w1'], 'L1_gnn_root1': _L1_gnn_in['root1'], 'L1_gnn_bias1': _L1_gnn_in['bias1'], 'L1_gnn_basis2': _L1_gnn_in['basis2'], 'L1_gnn_att2': _L1_gnn_in['att2'], 'L1_gnn_gate_w2': _L1_gnn_in['gate_w2'], 'L1_gnn_root2': _L1_gnn_in['root2'], 'L1_gnn_bias2': _L1_gnn_in['bias2']}

def reference(x, src, dst, edge_type_2, edge_type_32, edge_weight1, L0_gnn_bases, L0_gnn_w_comp, L0_gnn_h_bias, L1_gnn_basis1, L1_gnn_att1, L1_gnn_gate_w1, L1_gnn_root1, L1_gnn_bias1, L1_gnn_basis2, L1_gnn_att2, L1_gnn_gate_w2, L1_gnn_root2, L1_gnn_bias2):
    import jax
    import jax.numpy as jnp

    def _L0_gnn_ref(x, bases, w_comp, h_bias, norm, src, dst, etype):
        import jax, jax.numpy as jnp
        import numpy as np
        N_NODES = 2500
        N_EDGES = 40000
        IN_FEAT = 512
        OUT_FEAT = 512
        NUM_RELS = 32
        NUM_BASES = 8
        n_nodes = x.shape[0]
        weight = jnp.einsum('rb,bio->rio', w_comp, bases)
        h_rel = jnp.einsum('ni,rio->rno', x, weight)
        msg = h_rel[etype, src] * norm
        out = jax.ops.segment_sum(msg, dst, num_segments=n_nodes)
        out = out + h_bias
        return out

    def _L1_gnn_ref(x, edge_index, edge_type, basis1, att1, gate_w1, root1, bias1, basis2, att2, gate_w2, root2, bias2):
        import jax, jax.numpy as jnp
        import numpy as np
        NUM_RELATIONS = 2
        NUM_BASES = 30
        HIDDEN = 512
        N_NODES = 1250
        N_EDGES = 20000

        def rgcn_gate_layer(x, row, col, edge_type, basis, att, gate_w, root, bias):
            H = x.shape[1]
            w = jnp.einsum('rb,bio->rio', att, basis)
            x_j = x[col]
            msgs = []
            for r in range(NUM_RELATIONS):
                gate = jax.nn.sigmoid(x_j @ gate_w[r, :, 0])
                msgs.append(gate[:, None] * x_j @ w[r])
            msg = jnp.where((edge_type == 0)[:, None], msgs[0], msgs[1])
            agg = jax.ops.segment_sum(msg, row, num_segments=x.shape[0])
            return agg + x @ root + bias
        row, col = (edge_index[0], edge_index[1])
        h = jax.nn.relu(rgcn_gate_layer(x, row, col, edge_type, basis1, att1, gate_w1, root1, bias1))
        out = rgcn_gate_layer(h, row, col, edge_type, basis2, att2, gate_w2, root2, bias2)
        return out
    edge_index = jnp.stack([src, dst])
    h = jnp.maximum(_layernorm(x, axis=-1), 0.0)
    x = x + _L0_gnn_ref(h, L0_gnn_bases, L0_gnn_w_comp, L0_gnn_h_bias, edge_weight1, src, dst, edge_type_32)
    h = jnp.maximum(_layernorm(x, axis=-1), 0.0)
    x = x + _L1_gnn_ref(h, edge_index, edge_type_2, L1_gnn_basis1, L1_gnn_att1, L1_gnn_gate_w1, L1_gnn_root1, L1_gnn_bias1, L1_gnn_basis2, L1_gnn_att2, L1_gnn_gate_w2, L1_gnn_root2, L1_gnn_bias2)
    return x

_drawn_inputs = setup_inputs


def setup_inputs(seed=0):
    import zlib

    import numpy as np

    out = dict(_drawn_inputs(seed))
    spreads = {'L0_gnn_h_bias': (0.0, 0.1)}
    factors = {'L1_gnn_basis1': 8.0,
     'L1_gnn_att1': 8.0,
     'L1_gnn_gate_w1': 8.0,
     'L1_gnn_root1': 8.0,
     'L1_gnn_bias1': 27.211,
     'L1_gnn_basis2': 8.0,
     'L1_gnn_att2': 8.0,
     'L1_gnn_gate_w2': 31.882,
     'L1_gnn_root2': 8.0,
     'L1_gnn_bias2': 27.987}
    for name, (base, spread) in spreads.items():
        noise = np.random.default_rng([zlib.crc32(name.encode()), seed]).standard_normal(out[name].shape)
        drawn = base * np.exp(spread * noise) if base else spread * noise
        out[name] = jnp.asarray(drawn.astype(out[name].dtype))
    for name, factor in factors.items():
        out[name] = (out[name] * factor).astype(out[name].dtype)
    return out
```

```python
from contextlib import ExitStack

import concourse.bass as bass
from concourse import mybir

F32 = mybir.dt.float32
F16 = mybir.dt.float16
BF16 = mybir.dt.bfloat16
I32 = mybir.dt.int32
ALU = mybir.AluOpType
ACT = mybir.ActivationFunctionType

P = 128
N = 1250
D = 512
E = 20000
KC = D // P
NW = -(-N // P)
LAST = N - (NW - 1) * P
EP, ET = 125, 160
BASES = 8
TYPES = 32
RELS = 2
ATT = 30
LAYERS = 2
BN = P // BASES
NB = -(-N // BN)
GROUP = 4
AHEAD = 2 * GROUP
SLOTS = 8
SLOTS1 = 12
IDX = 12
PE_TILES = 8
FETCHES = 24
TC = 8
CHUNKS = ET // TC
PARTS = 5
PARTS1 = 2
BANKS = 8
BANK = 512
WRING = 3
OPEN_BANKS = 4
MIX_STEPS = 16
MIX_ROWS = 4 * MIX_STEPS
MIX_GROUPS = 6
MIX_EARLY = 4
MIX_LOAD = 4
MIX_PARTS = MIX_STEPS // MIX_LOAD
MRING = 4
MIX_CHUNKS = MIX_GROUPS * MIX_ROWS // P
MIX_HALF = (LAYERS * KC - MIX_CHUNKS) // 2 + 1
HALF = NW // 2
EPS = 1e-5


def tiles_for(buckets):
    worst = (E + buckets * (P - 1)) // P
    return -(-worst // FETCHES) * FETCHES


T0 = tiles_for(NB)
T1 = tiles_for(NW)
ds = bass.ds


def rows(w):
    return LAST if w == NW - 1 else P


class Space:

    def __init__(self, base, start=0, end=None):
        self.base, self.at, self.end = base, start, end if end is not None else base.shape[1]

    def words(self, n, parts=P, dt=F32):
        assert self.at + n <= self.end, (self.at, n, self.end)
        got = self.base[0:parts, self.at:self.at + n]
        self.at += n
        return got if dt == F32 else got.bitcast(dt)

    def halves(self, n, dt, parts=P):
        return self.words(-(-n // 2), parts, dt)[:, 0:n]


class Order:

    def __init__(self, nb, tiles, space, bank, bank_sums):
        self.nb, self.tiles = nb, tiles
        cube = nb * ET
        self.hot = space.halves(cube, F16, EP)
        self.count = space.halves(cube, F16, EP)
        self.base = space.halves(cube, F16, EP)
        self.key = space.halves(ET, F16, EP)
        self.slot_q = space.words(ET, EP)
        self.slot_r = space.halves(ET, F16, EP)
        self.int_a = space.words(ET, EP, I32)
        self.int_b = space.words(ET, EP, I32)
        self.ends = space.words(nb + 1, EP)
        self.own = space.halves(nb, BF16, EP)
        self.nt_i = space.words(nb, EP, I32)
        self.nt = space.words(nb, EP)
        self.upto = space.words(nb, EP)
        self.low = space.halves(nb, F16, EP)
        self.high = space.halves(nb, F16, EP)
        self.before = space.words(nb, EP)
        self.col_i = space.words(1, nb, I32)
        self.col_nt = space.halves(1, BF16, nb)
        self.col_end = space.words(1, nb)
        self.past = space.halves(tiles, BF16, nb)
        self.p_before = bank[0:EP, 0:nb]
        self.p_total = bank[0:EP, P:P + nb]
        self.p_down = bank[0:nb, 2 * P - 2:2 * P - 1]
        self.p_end = bank[0:nb, 2 * P - 1:2 * P]
        self.p_bucket = bank[0:1, 2 * P:2 * P + tiles]
        self.p_low = bank_sums[0:EP, 0:ET]
        self.p_high = bank_sums[0:EP, ET:2 * ET]


def part_of(words, field):
    return words.bitcast(field.dtype).rearrange("p (r t) -> p r t", t=TC)


def by_bucket(ap, nb):
    return ap.rearrange("p (k t) -> p k t", k=nb)


def gnn(nc, x, src, dst, edge_type_2, edge_type_32, edge_weight1, bases0, w_comp, h_bias,
        basis, att, gate_w, root, bias, out):
    with ExitStack() as ctx:
        def sb(name, shape, dt=F32):
            return ctx.enter_context(nc.sbuf_tensor(name, shape, dt))

        def sem(name):
            return ctx.enter_context(nc.semaphore(name))

        psum = ctx.enter_context(nc.psum_tensor("psum", [P, BANKS, BANK], F32))

        arena = sb("arena", [P, NB * D])
        region_x = sb("region_x", [P, NW * D])
        region_w = sb("region_w", [P, 4096])

        ident = sb("ident", [P, P])
        ident_b = sb("ident_b", [P, P], BF16)
        before_b = sb("before_b", [P, P], BF16)
        ones_b = sb("ones_b", [P, P], BF16)
        zeros_b = sb("zeros_b", [P, P], BF16)
        count1 = sb("count1", [P, P])
        count_t = sb("count_t", [P, T0], F16)
        ones_row = sb("ones_row", [1, P])
        att_row = sb("att_row", [1, LAYERS * RELS * ATT])
        att_all = sb("att_all", [P, LAYERS * RELS * ATT])
        gate_rows = sb("gate_rows", [LAYERS * RELS * KC, P])
        gates = sb("gates", [P, LAYERS, RELS, KC])
        row_grid = sb("row_grid", [P, P * TC], F16)
        comp = sb("comp", [P, GROUP * BASES])
        comp_rest = sb("comp_rest", [P, GROUP * BASES])
        comp_part = [sb(f"comp_part{i}", [P, GROUP * BASES], BF16) for i in range(3)]
        stats = sb("stats", [P, NW, 6])
        moments = sb("moments", [P, NW, 2])
        scale = sb("scale", [P, NW])
        shift = sb("shift", [P, NW])
        source = sb("source", [P, T0 + IDX], I32)
        place = sb("place", [P, T0 + AHEAD])
        kind = sb("kind", [P, T0 + AHEAD])
        weight = sb("weight", [P, T0 + AHEAD])
        bucket = sb("bucket", [1, T0], I32)
        index_slots = sb("index_slots", [P, FETCHES], I32)
        kind_hot = sb("kind_hot", [P, GROUP, TYPES], BF16)
        kind_hot_t = sb("kind_hot_t", [P, P], BF16)
        place_hot = sb("place_hot", [P, GROUP, BN])
        factor = sb("factor", [P, GROUP, BASES])

        x_sb = region_x[:].rearrange("p (w d) -> p w d", d=D)
        rx = Space(region_x)
        ring0 = rx.words(SLOTS * D).rearrange("p (s d) -> p s d", d=D)
        factors = rx.words(2 * GROUP * P).rearrange("p (g j c) -> p g j c", g=2, j=GROUP)

        def carrying_set(space, parts, tiles):
            return (space.halves(P * TC, F16, EP).rearrange("p (r t) -> p r t", t=TC),
                    [space.words(P * TC // 2, EP) for _ in range(parts)],
                    space.halves(TC * tiles, BF16, EP).rearrange("p (t q) -> p t q", t=TC))

        rx = Space(region_x)
        sets0 = [carrying_set(rx, PARTS, T0), carrying_set(Space(region_w), PARTS, T0)]

        a0 = Space(arena)
        h_out = a0.words(NW * D).rearrange("p (w d) -> p w d", d=D)
        early = a0.at + 3 * NB * ET // 2
        order0 = Order(NB, T0, a0, psum[:, 0, :], psum[:, 1, :])
        e_dst, e_src, e_kind = (a0.words(ET, EP, I32) for _ in range(3))
        e_weight, e_rest, e_place = (a0.words(ET, EP) for _ in range(3))
        e_int = a0.words(ET, EP, I32)
        f_source, f_code = a0.halves(ET, F16, EP), a0.halves(ET, F16, EP)
        f_weight = [a0.halves(ET, BF16, EP) for _ in range(3)]
        s_int = a0.words(T0, P, I32)
        s_int_b = a0.words(T0, P, I32)
        mix_at = a0.at
        mix_load = a0.words(MRING * MIX_LOAD * D, 4 * ATT).rearrange("p (g s d) -> p g s d", g=MRING, s=MIX_LOAD)
        mix_out = a0.words(2 * D).rearrange("p (g d) -> p g d", g=2)
        mix_att = a0.words(MIX_STEPS - 1 + P, 4 * ATT)
        used = a0.at

        sums = arena[:].rearrange("p (c m) -> p c m", c=KC)

        rw = Space(region_w)
        base_ring = rw.words(2 * D).rearrange("p (s d) -> p s d", s=2)
        basis_ring = rw.words(WRING * D).rearrange("p (s d) -> p s d", s=WRING)
        mix = rw.words(RELS * D).rearrange("p (r d) -> p r d", r=RELS)
        bias_row = rw.words(D, 1)

        a1 = Space(arena)
        h_n = a1.words(NW * D).rearrange("p (w d) -> p w d", d=D)
        h_t = a1.words(KC * NW * P).rearrange("p (c n) -> p c n", c=KC)
        w_sb = a1.words(RELS * KC * D).rearrange("p (r c d) -> p r c d", r=RELS, c=KC)
        root_sb = a1.words(KC * D).rearrange("p (c d) -> p c d", c=KC)
        acc_flat = a1.words(NW * D)
        acc = acc_flat.rearrange("p (w d) -> p w d", d=D)
        gated = a1.words(2 * RELS * D).rearrange("p (b r d) -> p b r d", b=2, r=RELS)
        gate = a1.words(RELS * NW).rearrange("p (w r) -> p w r", r=RELS)
        slot_hot = a1.words(PE_TILES * P).rearrange("p (s m) -> p s m", s=PE_TILES)
        row_of = a1.words(T1 + IDX, P, I32)
        local = a1.words(T1 + OPEN_BANKS)
        window = a1.words(T1, 1, I32)
        a2 = Space(arena, a1.at)
        ring1 = a1.words(SLOTS1 * D).rearrange("p (s d) -> p s d", d=D)
        order1 = Order(NW, T1, a2, psum[:, 0, :], psum[:, 1, :])
        g_dst, g_src, g_rel = (a2.words(ET, EP, I32) for _ in range(3))
        g_place = a2.words(ET, EP)
        g_row, g_code = a2.halves(ET, F16, EP), a2.halves(ET, F16, EP)
        sets1 = [carrying_set(a2, PARTS1, T1), carrying_set(a2, PARTS1, T1)]
        t_int = a2.words(T1, P, I32)
        t_int_b = a2.words(T1, P, I32)
        t_f = a2.words(T1)

        h_table = nc.dram_tensor("h_table", [N, D], F32).ap()
        gated_table = nc.dram_tensor("gated_table", [RELS * N, D], F32).ap()
        w_table = nc.dram_tensor("w_table", [LAYERS, RELS, D, D], F32).ap()

        ld_edges, ld_x, ld_small, ld_x2 = sem("ld_edges"), sem("ld_x"), sem("ld_small"), sem("ld_x2")
        ld_edges1, ld_bias = sem("ld_edges1"), [sem(f"ld_bias{i}") for i in range(LAYERS)]
        ld_bias_first = sem("ld_bias_first")
        ld_base = [sem(f"ld_base{i}") for i in range(2)]
        ld_basis = [sem(f"ld_basis{i}") for i in range(WRING)]
        ld_w = [sem(f"ld_w{i}") for i in range(LAYERS)]
        st_h, st_mix = sem("st_h"), sem("st_mix")
        st_gated = [sem(f"st_gated{i}") for i in range(2)]
        st_out = sem("st_out")
        fetched = [sem(f"fetched{i}") for i in range(SLOTS)]
        fetched1 = [sem(f"fetched1_{i}") for i in range(SLOTS1)]
        ld_att, ld_mix = sem("ld_att"), [sem(f"ld_mix{i}") for i in range(MRING)]
        st_first = [sem(f"st_first{i}") for i in range(2)]
        mix_read = sem("mix_read")
        mix_copied = sem("mix_copied")
        consts = sem("consts")
        cleared = sem("cleared")
        dve = sem("dve")
        prepared = sem("prepared")
        zeroed = sem("zeroed")
        counted = sem("counted")
        total = sem("total")
        tiles_down = sem("tiles_down")
        ends_down = sem("ends_down")
        past_made = sem("past_made")
        bucket_sum = sem("bucket_sum")
        split = sem("split")
        slot_sum = sem("slot_sum")
        carry_made = [sem(f"carry_made{i}") for i in range(2)]
        carried = [sem(f"carried{i}") for i in range(2)]
        row_hot_made = sem("row_hot_made")
        slots_known = sem("slots_known")
        att_spread = sem("att_spread")
        factor_step = sem("factor_step")
        carry_end = sem("carry_end")
        x_stats, x_scaled = sem("x_stats"), sem("x_scaled")
        rooted = sem("rooted")
        normed = sem("normed")
        window_made = sem("window_made")
        slots_made = sem("slots_made")
        hot_made = sem("hot_made")
        hot_turned = sem("hot_turned")
        hot_copied = sem("hot_copied")
        looked_up = sem("looked_up")
        factors_made = sem("factors_made")
        index_copied = sem("index_copied")
        pool_step = sem("pool_step")
        tile_done = sem("tile_done")
        tile_added = sem("tile_added")
        base_used = sem("base_used")
        layer0_done = sem("layer0_done")
        mixed = sem("mixed")
        x1_made = sem("x1_made")
        turned = sem("turned")
        turned_sb = sem("turned_sb")
        gate_sum = sem("gate_sum")
        gate_made = sem("gate_made")
        product = sem("product")
        product_sb = sem("product_sb")
        root_sum = sem("root_sum")
        root_in = sem("root_in")
        slots1_made = sem("slots1_made")
        slot_hot_made = sem("slot_hot_made")
        tile1_done = sem("tile1_done")
        tile1_added = sem("tile1_added")
        out_made = sem("out_made")
        index1_copied = sem("index1_copied")

        block = ctx.enter_context(nc.Block())

        def windows(dram, sbuf, engine, to_dram, signal):
            full, rest = dram[0:(NW - 1) * P, :].rearrange("(w p) d -> p w d", p=P), dram[(NW - 1) * P:N, :]
            for a, b in ((full, sbuf[:, 0:NW - 1, :]), (rest, sbuf[0:LAST, NW - 1, :])):
                engine.dma_start(a if to_dram else b, b if to_dram else a).then_inc(signal, 16)

        turn_bank = psum[:, 4, 0:P // 2].bitcast(BF16)
        edge_table = lambda a: a.rearrange("(p t) -> p t", p=EP)

        @block.sync
        def _(sp):
            sp.dma_start(e_dst, edge_table(dst)).then_inc(ld_edges, 16)
            sp.dma_start(e_src, edge_table(src)).then_inc(ld_edges, 16)
            sp.dma_start(e_kind, edge_table(edge_type_32)).then_inc(ld_edges, 16)
            sp.dma_start(e_weight, edge_weight1.rearrange("(p t) o -> p (t o)", p=EP)).then_inc(ld_edges, 16)
            sp.wait_ge(zeroed, 1)
            for r in range(RELS):
                for q in range(4):
                    at = MIX_STEPS - 1 + r * MIX_ROWS + q * MIX_STEPS
                    sp.dma_start(mix_att[q * ATT:(q + 1) * ATT, at:at + 1],
                                 att[0][r:r + 1, :].rearrange("r b -> b r")).then_inc(ld_att, 16)
            for n in range(MIX_GROUPS * MIX_PARTS):
                if n == MRING:
                    windows(x, x_sb, sp, False, ld_x)
                sp.wait_ge(mix_read, n + 1)
                for q in range(4):
                    row = n // MIX_PARTS * MIX_ROWS + q * MIX_STEPS + n % MIX_PARTS * MIX_LOAD
                    sp.dma_start(mix_load[q * ATT:(q + 1) * ATT, n % MRING], basis[0][:, row:row + MIX_LOAD, :]
                                 ).then_inc(ld_mix[n % MRING], 16)
            for j in range(GROUP):
                sp.dma_start(comp[TYPES * j:TYPES * (j + 1), BASES * j:BASES * (j + 1)], w_comp).then_inc(ld_small, 16)
            for layer in range(LAYERS):
                n = RELS * ATT
                sp.dma_start(att_row[0:1, layer * n:(layer + 1) * n],
                             att[layer].rearrange("(a r) b -> a (r b)", a=1)).then_inc(ld_small, 16)
                sp.dma_start(gate_rows[layer * RELS * KC:(layer + 1) * RELS * KC, :],
                             gate_w[layer].rearrange("r (c p) o -> (r c) (p o)", p=P)).then_inc(ld_small, 16)
            sp.wait_ge(normed, NW)
            windows(h_table, h_out, sp, True, st_h)

            sp.wait_ge(carry_end, 1)
            sp.dma_start(bias_row, h_bias.rearrange("(a d) -> a d", a=1)).then_inc(ld_bias_first, 16)

            sp.wait_ge(tile_added, 4 + T0)
            sp.wait_ge(factors_made, T0 // GROUP + 1)
            windows(x, x_sb, sp, False, ld_x2)
            for _half in range(2):
                with sp.Fori(0, BASES) as b:
                    for c in range(KC):
                        sp.wait_ge(base_used, b * KC + (_half * BASES * KC + c + 1))
                        sp.dma_start(base_ring[:, c % 2, :],
                                     bases0[ds(b, 1), c * P:(c + 1) * P, :].rearrange("b i o -> i (b o)")
                                     ).then_inc(ld_base[c % 2], 16)

            for layer in range(LAYERS):
                if layer == 0:
                    sp.wait_ge(layer0_done, NW)
                    sp.wait_ge(st_mix, 16 * (LAYERS * KC - MIX_CHUNKS))
                    for i in range(2):
                        sp.wait_ge(st_first[i], 16 * RELS * MIX_GROUPS // 2)
                    for dram, sbuf in ((dst, g_dst), (src, g_src), (edge_type_2, g_rel)):
                        sp.dma_start(sbuf, edge_table(dram)).then_inc(ld_edges1, 16)
                else:
                    sp.wait_ge(root_sum, NW)
                for r in range(RELS):
                    sp.dma_start(w_sb[:, r], w_table[layer, r].rearrange("(c p) o -> p c o", p=P)).then_inc(ld_w[layer], 16)
                sp.dma_start(root_sb, root[layer].rearrange("(c p) o -> p c o", p=P)).then_inc(ld_w[layer], 16)
                sp.dma_start(bias_row, bias[layer].rearrange("(a d) -> a d", a=1)).then_inc(ld_bias[layer], 16)
                if layer == 1:
                    sp.wait_ge(tile1_done, SLOTS1 + T1)
                for w in range(NW):
                    for r in range(RELS):
                        sp.wait_ge(product_sb, (layer * NW + w) * RELS + r + 1)
                        sp.dma_start(gated_table[r * N + w * P:r * N + w * P + rows(w), :],
                                     gated[0:rows(w), w % 2, r, :]).then_inc(st_gated[w % 2], 16)

            for w in range(NW):
                sp.wait_ge(out_made, w + 1)
                sp.dma_start(out[w * P:w * P + rows(w), :], x_sb[0:rows(w), w, :]).then_inc(st_out, 16)
            sp.wait_ge(st_out, 16 * NW)

        @block.gpsimd
        def _(pool):
            pool.iota(count1[:], [[1, P]], base=1, channel_multiplier=0,
                      allow_small_or_imprecise_dtypes=True).then_inc(consts, 1)
            pool.iota(count_t[:], [[1, T0]], base=0, channel_multiplier=0,
                      allow_small_or_imprecise_dtypes=True).then_inc(consts, 1)
            pool.iota(row_grid[:].rearrange("p (r t) -> p r t", t=TC), [[1, P], [0, TC]], base=0, channel_multiplier=0,
                      allow_small_or_imprecise_dtypes=True).then_inc(consts, 1)
            pool.memset(ident[:], 0.0).then_inc(pool_step, 1)
            pool.memset(before_b[:], 1.0).then_inc(pool_step, 1)
            pool.wait_ge(pool_step, 2)
            pool.affine_select(out=ident[:], in_=ident[:], compare_op=ALU.not_equal, fill=1.0, base=0,
                               pattern=[[-1, P]], channel_multiplier=1).then_inc(consts, 1)
            pool.affine_select(out=before_b[:], in_=before_b[:], compare_op=ALU.is_gt, fill=0.0, base=0,
                               pattern=[[1, P]], channel_multiplier=-1).then_inc(consts, 1)

            pool.memset(arena[:, used:], 0.0).then_inc(cleared, 1)
            pool.wait_ge(slots_known, 1)
            pool.wait_ge(st_h, 32)
            pool.memset(arena[:, 0:early], 0.0).then_inc(cleared, 1)
            for i in range(2):
                pool.wait_ge(st_first[i], 16 * RELS * MIX_GROUPS // 2)
            pool.memset(arena[:, mix_at:used], 0.0).then_inc(cleared, 1)
            pool.wait_ge(slots_made, 1)
            pool.memset(arena[:, early:mix_at], 0.0).then_inc(cleared, 1)

            def fetch(table, index, slots, ring, done, freed, tiles, copied, base):
                half = lambda h: index_slots[:, h * IDX:(h + 1) * IDX]
                copies = base // tiles * (2 * tiles // FETCHES + 1)
                if copies:
                    pool.wait_ge(copied, copies)
                pool.tensor_copy(half(0), index[:, 0:IDX]).then_inc(copied, 1)
                with pool.Fori(0, tiles // FETCHES) as i:
                    for k in range(FETCHES):
                        if k % 2 == 0:
                            pool.wait_ge(freed, i * FETCHES + (base + k + 2))
                            pool.sem_inc(pool_step, 1)
                        if k % IDX == IDX - 2:
                            pool.tensor_copy(half((k // IDX + 1) % 2), index[:, ds(i * FETCHES + (k // IDX + 1) * IDX, IDX)]
                                             ).then_inc(copied, 1)
                        if k % IDX == 0:
                            pool.wait_ge(copied, i * 2 + (k // IDX + 1 + copies))
                            pool.sem_inc(pool_step, 1)
                        pool.indirect_dma_start(ring[:, k % slots, :], None, table,
                                                bass.IndirectOffsetOnAxis(index_slots[:, k:k + 1], 0)
                                                ).then_inc(done[k % slots], 16)

            fetch(h_table, source, SLOTS, ring0, fetched, tile_done, T0, index_copied, 0)

            pool.wait_ge(index_copied, 2 * T0 // FETCHES + 1)
            pool.wait_ge(slots1_made, 1)
            for layer in range(LAYERS):
                for half in range(2):
                    pool.wait_ge(st_gated[half], 16 * (layer + 1) * RELS * (NW // 2))
                fetch(gated_table, row_of, SLOTS1, ring1, fetched1, tile1_done, T1, index1_copied, layer * T1)

        @block.scalar
        def _(act):
            def store_mixed(groups):
                for g in groups:
                    act.wait_ge(mix_read, MRING + (g + 1) * MIX_PARTS)
                    if g >= 2:
                        act.wait_ge(st_first[g % 2], 16 * RELS * (g // 2))
                    nc.scalar.copy(mix_out[:, g % 2, :], psum[:, 7, :]).then_inc(mix_copied, 1)
                    act.wait_ge(mix_copied, g + 1)
                    for r in range(RELS):
                        act.dma_start(w_table[0, r, g * MIX_ROWS:(g + 1) * MIX_ROWS, :],
                                      mix_out[r * MIX_ROWS:(r + 1) * MIX_ROWS, g % 2, :]).then_inc(st_first[g % 2], 16)

            store_mixed(range(MIX_EARLY))
            act.wait_ge(x_stats, 1)
            nc.scalar.activation(scale[:], moments[:, :, 1], ACT.Sqrt).then_inc(rooted, 1)
            act.wait_ge(x_scaled, 1)
            for w in range(NW):
                nc.scalar.activation(h_out[:, w, :], x_sb[:, w, :], ACT.Relu, bias=shift[:, w:w + 1],
                                     scale=scale[:, w:w + 1]).then_inc(normed, 1)

            store_mixed(range(MIX_EARLY, MIX_GROUPS))
            act.wait_ge(hot_turned, 1)
            nc.scalar.copy(kind_hot_t[:], turn_bank).then_inc(hot_copied, 1)
            with act.Fori(0, T0 // GROUP + 1) as g:
                act.wait_ge(looked_up, g + 1)
                act.wait_ge(hot_turned, g + 2)
                nc.scalar.activation(kind_hot_t[:], turn_bank, ACT.Copy).then_inc(hot_copied, 1)

            for layer in range(LAYERS):
                for c in range(MIX_CHUNKS if layer == 0 else 0, KC):
                    block_at = layer * KC + c - MIX_CHUNKS
                    with act.Fori(0, ATT // WRING) as j:
                        for s in range(WRING):
                            act.wait_ge(mixed, j * (2 * WRING) + (block_at * ATT + s + 1) * RELS)
                            act.dma_start(basis_ring[:, s, :],
                                          basis[layer][ds(j * WRING + s, 1), c * P:(c + 1) * P, :].rearrange("b i o -> i (b o)")
                                          ).then_inc(ld_basis[s], 16)
                    act.wait_ge(mixed, 2 * WRING + (block_at + 1) * ATT * RELS)
                    act.dma_start(w_table[layer, :, c * P:(c + 1) * P, :].rearrange("r i o -> i r o"),
                                  mix).then_inc(st_mix, 16)

            act.wait_ge(x_stats, 2)
            nc.scalar.activation(scale[:], moments[:, :, 1], ACT.Sqrt).then_inc(rooted, 1)
            act.wait_ge(x_scaled, 2)
            for w in range(NW):
                nc.scalar.activation(h_n[0:rows(w), w, :], x_sb[0:rows(w), w, :], ACT.Relu,
                                     bias=shift[0:rows(w), w:w + 1], scale=scale[0:rows(w), w:w + 1]).then_inc(normed, 1)

            for layer in range(LAYERS):
                for w in range(NW):
                    act.wait_ge(turned, layer * NW + w + 1)
                    nc.scalar.activation(h_t[:, :, w * P:w * P + rows(w)],
                                         psum[:, 2 + w % 2, :].rearrange("p (c n) -> p c n", c=KC)[:, :, 0:rows(w)],
                                         ACT.Relu).then_inc(turned_sb, 1)
                act.wait_ge(gate_sum, layer + 1)
                gate_bank = psum[:, 7, 0:RELS * NW].rearrange("p (w r) -> p w r", r=RELS)
                nc.scalar.activation(gate[:, 0:NW - 1, :], gate_bank[:, 0:NW - 1, :], ACT.Sigmoid).then_inc(gate_made, 1)
                nc.scalar.activation(gate[0:LAST, NW - 1, :], gate_bank[0:LAST, NW - 1, :], ACT.Sigmoid).then_inc(gate_made, 1)
                act.wait_ge(gate_made, 2 * layer + 2)
                for w in range(NW):
                    for r in range(RELS):
                        n = (layer * NW + w) * RELS + r
                        act.wait_ge(product, n + 1)
                        if r == 0 and layer * NW + w >= 2:
                            act.wait_ge(st_gated[w % 2], 16 * RELS * ((layer * NW + w) // 2))
                        nc.scalar.activation(gated[0:rows(w), w % 2, r, :], psum[0:rows(w), 2 + n % 4, :], ACT.Copy,
                                             scale=gate[0:rows(w), w, r:r + 1]).then_inc(product_sb, 1)
                for w in range(NW):
                    act.wait_ge(root_sum, layer * NW + w + 1)
                    nc.scalar.copy(acc[0:rows(w), w, :], psum[0:rows(w), 6 + w % 2, :]).then_inc(root_in, 1)

        @block.vector
        def _(eng):
            v = nc.vector
            steps = {}

            def chain(ins, signal=dve):
                steps[signal.name] = steps.get(signal.name, 0) + 1
                ins.then_inc(signal, 1)
                eng.wait_ge(signal, steps[signal.name])

            def place_edges(o, n):
                hot, count, base = (by_bucket(a, o.nb) for a in (o.hot, o.count, o.base))
                over = lambda a: a.unsqueeze(2).broadcast_to((EP, o.nb, ET))
                chain(v.tensor_tensor(hot, o.key.unsqueeze(1).broadcast_to((EP, o.nb, ET)), over(count_t[0:EP, 0:o.nb]),
                                      ALU.is_equal))
                chain(v.tensor_tensor_scan(o.count, o.hot, o.hot, 0.0, ALU.add, ALU.max))
                chain(v.memset(o.ends[:, 0:1], 0.0))
                chain(v.tensor_copy(o.ends[:, 1:o.nb + 1], count[:, :, ET - 1]))
                chain(v.tensor_tensor(o.own, o.ends[:, 1:o.nb + 1], o.ends[:, 0:o.nb], ALU.subtract), counted)
                eng.wait_ge(total, n + 1)
                chain(v.tensor_scalar(o.col_i, o.p_down, float(P - 1), None, ALU.add))
                chain(v.tensor_scalar(o.nt_i, o.p_total, float(P - 1), None, ALU.add))
                chain(v.tensor_scalar(o.col_i, o.col_i, 7, None, ALU.arith_shift_right))
                chain(v.tensor_scalar(o.nt_i, o.nt_i, 7, None, ALU.arith_shift_right))
                chain(v.tensor_copy(o.nt, o.nt_i))
                chain(v.tensor_copy(o.before, o.p_before))
                chain(v.tensor_copy(o.col_nt, o.col_i), tiles_down)
                chain(v.tensor_tensor_scan(o.upto, o.nt, o.nt, 0.0, ALU.add, ALU.max))
                chain(v.tensor_tensor(o.upto, o.upto, o.nt, ALU.subtract))
                chain(v.scalar_tensor_tensor(o.upto, o.upto, float(P), o.before, ALU.mult, ALU.add))
                chain(v.tensor_tensor(o.upto, o.upto, o.ends[:, 0:o.nb], ALU.subtract))
                chain(v.tensor_copy(o.nt_i, o.upto))
                chain(v.tensor_scalar(o.nt_i, o.nt_i, P - 1, None, ALU.bitwise_and))
                chain(v.tensor_copy(o.low, o.nt_i))
                chain(v.tensor_copy(o.nt_i, o.upto))
                chain(v.tensor_scalar(o.nt_i, o.nt_i, 7, None, ALU.arith_shift_right))
                chain(v.tensor_copy(o.high, o.nt_i))
                chain(v.tensor_tensor(count, count, over(o.low), ALU.add))
                chain(v.tensor_tensor(o.count, o.count, o.hot, ALU.mult))
                chain(v.tensor_tensor(base, hot, over(o.high), ALU.mult), split)
                eng.wait_ge(ends_down, n + 1)
                chain(v.tensor_copy(o.col_end, o.p_end))
                chain(v.tensor_scalar(o.past, count_t[0:o.nb, 0:o.tiles], o.col_end, None, ALU.is_ge), past_made)

            def slots_of_edges(o, n):
                eng.wait_ge(slot_sum, n + 1)
                chain(v.tensor_scalar(o.int_a, o.p_low, 1.0, None, ALU.subtract))
                chain(v.tensor_scalar(o.int_b, o.int_a, P - 1, None, ALU.bitwise_and))
                chain(v.tensor_copy(o.slot_r, o.int_b))
                chain(v.tensor_scalar(o.int_a, o.int_a, 7, None, ALU.arith_shift_right))
                chain(v.tensor_tensor(o.slot_q, o.p_high, o.int_a, ALU.add), slots_known)

            def carry_edges(o, sets, fields, n):
                grid = row_grid[0:EP, :].rearrange("p (r t) -> p r t", t=TC)
                with eng.Fori(0, CHUNKS // 2) as i:
                    for k in range(2):
                        row_hot, row_parts, tile_hot = sets[k]
                        col = (i * 2 + k) * TC
                        eng.wait_ge(carried[k], i + (n * (CHUNKS // 2) + 1))
                        v.tensor_tensor(row_hot, grid, o.slot_r[:, ds(col, TC)].unsqueeze(1).broadcast_to((EP, P, TC)),
                                        ALU.is_equal).then_inc(row_hot_made, 1)
                        for t in range(TC):
                            v.tensor_scalar(tile_hot[:, t, :], count_t[0:EP, 0:o.tiles], o.slot_q[:, ds(col + t, 1)], None,
                                            ALU.is_equal)
                        eng.wait_ge(row_hot_made, i * 2 + (k + 1 + n * CHUNKS))
                        for part, field in zip(row_parts, fields):
                            last = v.tensor_tensor(part_of(part, field), row_hot,
                                                   field[:, ds(col, TC)].unsqueeze(1).broadcast_to((EP, P, TC)), ALU.mult)
                        last.then_inc(carry_made[k], 1)

            def norm_statistics(limit):
                for w in range(NW):
                    last = v.bn_stats(stats[0:limit(w), w, :], x_sb[0:limit(w), w, :])
                chain(last)
                for w in range(NW):
                    last = v.bn_aggr(moments[0:limit(w), w, :], stats[0:limit(w), w, :])
                chain(last)
                chain(v.tensor_scalar(moments[:, :, 1], moments[:, :, 1], EPS, None, ALU.add), x_stats)

            def norm_scales(n):
                eng.wait_ge(rooted, n)
                chain(v.reciprocal(scale[:], scale[:]))
                chain(v.scalar_tensor_tensor(shift[:], moments[:, :, 0], -1.0, scale[:], ALU.mult, ALU.mult), x_scaled)

            v.memset(comp[:], 0.0)
            v.memset(mix_att, 0.0)
            v.memset(x_sb[:, NW - 1, :], 0.0).then_inc(zeroed, 1)
            v.memset(ones_b[:], 1.0)
            v.memset(zeros_b[:], 0.0)
            v.memset(ones_row[:], 1.0)
            v.memset(source[:], 0)
            for a in (place, kind, weight):
                v.memset(a[:], 0.0)
            eng.sem_inc(tile_added, OPEN_BANKS)
            eng.sem_inc(tile1_added, OPEN_BANKS)
            eng.sem_inc(mixed, 2 * WRING)
            eng.wait_ge(consts, 5)
            chain(v.tensor_copy(ident_b[:], ident[:]), prepared)

            eng.wait_ge(ld_edges, 64)
            chain(v.tensor_scalar(e_int, e_dst, 4, None, ALU.arith_shift_right))
            chain(v.tensor_copy(order0.key, e_int))
            place_edges(order0, 0)
            chain(v.tensor_copy(f_source, e_src))
            chain(v.tensor_scalar(e_int, e_dst, BN - 1, None, ALU.bitwise_and))
            chain(v.tensor_scalar(e_place, e_int, float(TYPES), None, ALU.mult))
            chain(v.tensor_tensor(f_code, e_place, e_kind, ALU.add))
            chain(v.tensor_copy(f_weight[0], e_weight))
            chain(v.tensor_tensor(e_rest, e_weight, f_weight[0], ALU.subtract))
            chain(v.tensor_copy(f_weight[1], e_rest))
            chain(v.tensor_tensor(e_rest, e_rest, f_weight[1], ALU.subtract))
            chain(v.tensor_copy(f_weight[2], e_rest))
            eng.wait_ge(ld_x, 32)
            norm_statistics(lambda w: P)
            slots_of_edges(order0, 0)
            norm_scales(1)
            eng.wait_ge(normed, NW)
            carry_edges(order0, sets0, [f_source, f_code, *f_weight], 0)
            eng.wait_ge(ld_small, 16 * (GROUP + 2 * LAYERS))
            chain(v.tensor_copy(comp_part[0][:], comp[:]))
            chain(v.tensor_tensor(comp_rest[:], comp[:], comp_part[0][:], ALU.subtract))
            chain(v.tensor_copy(comp_part[1][:], comp_rest[:]))
            chain(v.tensor_tensor(comp_rest[:], comp_rest[:], comp_part[1][:], ALU.subtract))
            chain(v.tensor_copy(comp_part[2][:], comp_rest[:]), prepared)
            eng.wait_ge(att_spread, 1)
            chain(v.tensor_copy(att_all[:], psum[:, 7, 0:LAYERS * RELS * ATT]))
            chain(v.tensor_copy(gates[:].rearrange("p l r c -> p (l r c)"), psum[:, 7, P:P + LAYERS * RELS * KC]))
            eng.wait_ge(bucket_sum, 1)
            chain(v.tensor_scalar(bucket[:], order0.p_bucket, float(NB - 1), None, ALU.min))
            eng.wait_ge(carry_end, 1)
            chain(v.tensor_copy(source[:, 0:T0], psum[:, 2, 0:T0]))
            chain(v.tensor_copy(s_int, psum[:, 3, 0:T0]))
            chain(v.tensor_scalar(s_int_b, s_int, 5, None, ALU.arith_shift_right))
            chain(v.tensor_copy(place[:, 0:T0], s_int_b))
            chain(v.tensor_scalar(s_int, s_int, TYPES - 1, None, ALU.bitwise_and))
            chain(v.tensor_copy(kind[:, 0:T0], s_int))
            chain(v.tensor_copy(weight[:, 0:T0], psum[:, 4, 0:T0]))
            chain(v.tensor_tensor(weight[:, 0:T0], weight[:, 0:T0], psum[:, 5, 0:T0], ALU.add))
            chain(v.tensor_tensor(weight[:, 0:T0], weight[:, 0:T0], psum[:, 6, 0:T0], ALU.add), slots_made)

            def kinds(g):
                v.tensor_tensor(kind_hot[:], kind[:, ds(g * GROUP, GROUP)].unsqueeze(2).broadcast_to((P, GROUP, TYPES)),
                                count_t[:, 0:TYPES].unsqueeze(1).broadcast_to((P, GROUP, TYPES)),
                                ALU.is_equal).then_inc(hot_made, 1)

            def make_factors(g, ahead):
                cols = ds(g * GROUP, GROUP)
                v.tensor_tensor(place_hot[:], place[:, cols].unsqueeze(2).broadcast_to((P, GROUP, BN)),
                                count_t[:, 0:BN].unsqueeze(1).broadcast_to((P, GROUP, BN)),
                                ALU.is_equal).then_inc(factor_step, 1)
                eng.wait_ge(looked_up, g + 1)
                v.tensor_tensor(factor[:], psum[:, 5, 0:GROUP * BASES].rearrange("p (j b) -> p j b", j=GROUP),
                                weight[:, cols].unsqueeze(2).broadcast_to((P, GROUP, BASES)),
                                ALU.mult).then_inc(factor_step, 1)
                eng.wait_ge(factor_step, g * 2 + 2)
                return v.tensor_tensor(factors[:, ahead].rearrange("p j (n b) -> p j n b", b=BASES),
                                       factor[:].unsqueeze(2).broadcast_to((P, GROUP, BN, BASES)),
                                       place_hot[:].unsqueeze(3).broadcast_to((P, GROUP, BN, BASES)),
                                       ALU.mult).then_inc(factors_made, 1)

            kinds(0)
            eng.wait_ge(hot_turned, 1)
            kinds(1)
            make_factors(0, 0)
            eng.wait_ge(cleared, 4)
            with eng.Fori(0, T0 // PE_TILES) as i, ExitStack() as held:
                regs = [held.enter_context(eng.register(f"bucket_{j}")) for j in range(PE_TILES)]
                eng.load(regs, bucket[0:1, ds(i * PE_TILES, PE_TILES)])
                for h in range(2):
                    g = i * 2 + h
                    eng.wait_ge(hot_turned, g + 2)
                    kinds(g + 2)
                    for j in range(GROUP):
                        k = GROUP * h + j
                        b = eng.snap(regs[k], min_val=0, max_val=NB - 1)
                        into = sums[:, :, ds(b * P, P)]
                        added, done = (eng.snap(i * PE_TILES + (k + n)) for n in (OPEN_BANKS, 1 + SLOTS))
                        eng.wait_ge(tile_done, done)
                        eng.wait_ge(tile_added, added)
                        v.tensor_tensor(into, into, psum[:, k % OPEN_BANKS, :].rearrange("p (c m) -> p c m", c=KC),
                                        ALU.add).then_inc(tile_added, 1)
                        if j == 0:
                            eng.wait_ge(tile_done, g * GROUP + SLOTS)
                            eng.wait_ge(factors_made, g + 1)
                            make_factors(g + 1, 1 - h)

            def mix_bases(chunks):
                for layer, c in chunks:
                    block_at = layer * KC + c - MIX_CHUNKS
                    if block_at:
                        eng.wait_ge(st_mix, 16 * block_at)
                    chain(v.memset(mix, 0.0))
                    with eng.Fori(0, ATT // WRING) as j:
                        for s in range(WRING):
                            eng.wait_ge(ld_basis[s], j * 16 + 16 * (block_at * (ATT // WRING) + 1))
                            for r in range(RELS):
                                eng.wait_ge(mixed, j * (WRING * RELS) + (block_at * ATT * RELS + RELS * s + r - 1 + 2 * WRING))
                                v.scalar_tensor_tensor(mix[:, r, :], basis_ring[:, s, :],
                                                       att_all[:, ds(j * WRING + ((layer * RELS + r) * ATT + s), 1)],
                                                       mix[:, r, :], ALU.mult, ALU.add).then_inc(mixed, 1)

            def add_layer0(half):
                for w in range(half * HALF, (half + 1) * HALF):
                    eng.wait_ge(layer0_done, w + 1)
                    chain(v.tensor_tensor(x_sb[0:rows(w), w, :], x_sb[0:rows(w), w, :], psum[0:rows(w), w % BANKS, :],
                                          ALU.add), x1_made)

            left = [(layer, c) for layer in range(LAYERS) for c in range(KC)][MIX_CHUNKS:]
            mix_bases(left[:MIX_HALF])
            eng.wait_ge(ld_x2, 32)
            add_layer0(0)
            mix_bases(left[MIX_HALF:])
            add_layer0(1)
            norm_statistics(rows)
            norm_scales(2)

            v.memset(local, 0.0)
            v.memset(row_of, 0)
            chain(v.memset(acc[:, NW - 1, :], 0.0), prepared)
            eng.wait_ge(ld_edges1, 48)
            chain(v.tensor_scalar(order1.int_a, g_src, 7, None, ALU.arith_shift_right))
            chain(v.tensor_copy(order1.key, order1.int_a))
            place_edges(order1, 1)
            chain(v.tensor_copy(g_row, g_dst))
            chain(v.tensor_scalar(order1.int_b, g_src, P - 1, None, ALU.bitwise_and))
            chain(v.tensor_scalar(g_place, order1.int_b, 1.0, 2.0, ALU.add, ALU.mult))
            chain(v.tensor_tensor(g_code, g_place, g_rel, ALU.add))
            slots_of_edges(order1, 1)
            eng.wait_ge(bucket_sum, 2)
            chain(v.tensor_scalar(window, order1.p_bucket, float(NW - 1), None, ALU.min), window_made)
            carry_edges(order1, sets1, [g_row, g_code], 1)
            eng.wait_ge(carry_end, 2)
            chain(v.tensor_copy(t_int, psum[:, 1, 0:T1]))
            chain(v.tensor_scalar(t_int_b, t_int, 1, None, ALU.arith_shift_right))
            chain(v.tensor_copy(local[:, 0:T1], t_int_b))
            chain(v.tensor_scalar(t_int, t_int, 1, None, ALU.bitwise_and))
            chain(v.tensor_scalar(t_f, t_int, float(N), None, ALU.mult))
            chain(v.tensor_tensor(row_of[:, 0:T1], t_f, psum[:, 0, 0:T1], ALU.add), slots1_made)

            def slot_matrix(n, k):
                v.tensor_scalar(slot_hot[:, k, :], count1[:], local[:, ds(n, 1)], None,
                                ALU.is_equal).then_inc(slot_hot_made, 1)

            for layer in range(LAYERS):
                if layer:
                    eng.wait_ge(slot_hot_made, layer * (T1 + OPEN_BANKS))
                for n in range(OPEN_BANKS):
                    slot_matrix(n, n)
                eng.wait_ge(root_in, (layer + 1) * NW)
                with eng.Fori(0, T1 // PE_TILES) as i, ExitStack() as held:
                    regs = [held.enter_context(eng.register(f"window_{layer}_{j}")) for j in range(PE_TILES)]
                    eng.load(regs, window[0:1, ds(i * PE_TILES, PE_TILES)])
                    for k in range(PE_TILES):
                        eng.wait_ge(tile1_done, i * PE_TILES + (layer * T1 + k - OPEN_BANKS + 1 + SLOTS1))
                        slot_matrix(i * PE_TILES + (k + OPEN_BANKS), (k + OPEN_BANKS) % PE_TILES)
                        at = eng.snap(regs[k], min_val=0, max_val=NW - 1)
                        into = acc_flat[:, ds(at * D, D)]
                        eng.wait_ge(tile1_added, i * PE_TILES + (layer * T1 + k + OPEN_BANKS))
                        eng.wait_ge(tile1_done, i * PE_TILES + (layer * T1 + k + 1 + SLOTS1))
                        v.tensor_tensor(into, into, psum[:, k % OPEN_BANKS, :], ALU.add).then_inc(tile1_added, 1)

            eng.wait_ge(tile1_added, LAYERS * T1 + OPEN_BANKS)
            for w in range(NW):
                v.tensor_tensor(x_sb[0:rows(w), w, :], x_sb[0:rows(w), w, :], acc[0:rows(w), w, :],
                                ALU.add).then_inc(out_made, 1)

        @block.tensor
        def _(pe):
            mm = nc.tensor.matmul
            pe.sem_inc(tile_done, SLOTS)
            pe.sem_inc(tile1_done, SLOTS1)
            pe.sem_inc(base_used, 2)
            pe.sem_inc(mix_read, MRING)
            for k in range(2):
                pe.sem_inc(carried[k], 1)

            def count_totals(o, n):
                pe.wait_ge(counted, n + 1)
                mm(o.p_before, before_b[0:EP, 0:EP], o.own, start=True, stop=True)
                mm(o.p_total, ones_b[0:EP, 0:EP], o.own, start=True, stop=True)
                mm(o.p_down, o.own, ones_b[0:EP, 0:1], start=True, stop=True).then_inc(total, 1)

            def count_tiles(o, n):
                pe.wait_ge(tiles_down, n + 1)
                mm(o.p_end, before_b[0:o.nb, 0:o.nb], o.col_nt, start=True, stop=False)
                mm(o.p_end, ident_b[0:o.nb, 0:o.nb], o.col_nt, start=False, stop=True).then_inc(ends_down, 1)

            def sum_buckets(o, n):
                pe.wait_ge(past_made, n + 1)
                mm(o.p_bucket, ones_b[0:o.nb, 0:1], o.past, start=True, stop=True).then_inc(bucket_sum, 1)

            def sum_slots(o, n):
                pe.wait_ge(split, n + 1)
                for out_, table in ((o.p_low, o.count), (o.p_high, o.base)):
                    for k in range(o.nb):
                        last = mm(out_, ident_b[0:EP, 0:EP], table[:, k * ET:(k + 1) * ET], start=(k == 0), stop=(k == o.nb - 1))
                last.then_inc(slot_sum, 1)

            def carry_open(banks, o, stop=False):
                for b in banks:
                    last = mm(psum[:, b, 0:o.tiles], zeros_b[0:EP, :], count_t[0:EP, 0:o.tiles], start=not stop, stop=stop,
                              skip_group_check=True)
                return last

            def carry_chunk(sets, fields, banks, o, k, ready):
                pe.wait_ge(carry_made[k], ready)
                _, row_parts, tile_hot = sets[k]
                for t in range(TC):
                    for part, field, b in zip(row_parts, fields, banks):
                        last = mm(psum[:, b, 0:o.tiles], part_of(part, field)[:, :, t], tile_hot[:, t, :],
                                  start=False, stop=False, skip_group_check=True)
                last.then_inc(carried[k], 1)

            def mix_steps(g, parts):
                for part in parts:
                    n = g * MIX_PARTS + part
                    pe.wait_ge(ld_mix[n % MRING], 64 * (n // MRING + 1))
                    if part == 0 and g:
                        pe.wait_ge(mix_copied, g)
                    for t in range(MIX_LOAD):
                        s = part * MIX_LOAD + t
                        last = mm(psum[:, 7, :], mix_att[:, MIX_STEPS - 1 - s:MIX_STEPS - 1 - s + P],
                                  mix_load[:, n % MRING, t, :], start=(s == 0), stop=(s == MIX_STEPS - 1))
                    last.then_inc(mix_read, 1)

            pe.wait_ge(ld_att, 16 * RELS * 4)
            mix_steps(0, range(MIX_PARTS))
            mix_steps(1, range(MIX_PARTS))
            pe.wait_ge(prepared, 1)
            count_totals(order0, 0)
            count_tiles(order0, 0)
            for g in range(2, MIX_EARLY):
                mix_steps(g, range(MIX_PARTS))
            sum_slots(order0, 0)
            sum_buckets(order0, 0)
            for g in range(MIX_EARLY, MIX_GROUPS):
                mix_steps(g, range(MIX_PARTS))
            fields0 = [f_source, f_code, *f_weight]
            banks0 = range(2, 2 + PARTS)
            carry_open(banks0, order0)
            with pe.Fori(0, CHUNKS // 2) as i:
                for k in range(2):
                    carry_chunk(sets0, fields0, banks0, order0, k, i + 1)
            carry_open(banks0, order0, stop=True).then_inc(carry_end, 1)
            pe.wait_ge(ld_small, 16 * (GROUP + 2 * LAYERS))
            pe.wait_ge(mix_copied, MIX_GROUPS)
            mm(psum[:, 7, 0:LAYERS * RELS * ATT], ones_row[:], att_row[:], start=True, stop=True)
            nc.tensor.transpose(psum[:, 7, P:P + LAYERS * RELS * KC], gate_rows[:],
                                ident[0:LAYERS * RELS * KC, 0:LAYERS * RELS * KC]).then_inc(att_spread, 1)

            def turn_kinds():
                nc.tensor.transpose(turn_bank, kind_hot[:].rearrange("p j k -> p (j k)"), ident_b[:]).then_inc(hot_turned, 1)

            def look_up():
                for k in range(3):
                    last = mm(psum[:, 5, 0:GROUP * BASES], kind_hot_t[:], comp_part[k][:], start=(k == 0), stop=(k == 2))
                last.then_inc(looked_up, 1)

            pe.wait_ge(slots_made, 1)
            pe.wait_ge(prepared, 2)
            pe.wait_ge(hot_made, 1)
            turn_kinds()
            pe.wait_ge(hot_made, 2)
            pe.wait_ge(hot_copied, 1)
            turn_kinds()
            look_up()
            with pe.Fori(0, T0 // PE_TILES) as i:
                for h in range(2):
                    g = i * 2 + h
                    pe.wait_ge(factors_made, g + 1)
                    for j in range(GROUP):
                        k = GROUP * h + j
                        pe.wait_ge(fetched[k], i * 16 + 16)
                        pe.wait_ge(tile_added, i * PE_TILES + (k + 1))
                        for c in range(KC):
                            last = mm(psum[:, k % OPEN_BANKS, c * P:(c + 1) * P], ring0[:, k, c * P:(c + 1) * P],
                                      factors[:, h, j, :], start=True, stop=True)
                        last.then_inc(tile_done, 1)
                        if j == 0:
                            pe.wait_ge(hot_copied, g + 2)
                            look_up()
                        elif j == 1:
                            pe.wait_ge(hot_made, g + 3)
                            turn_kinds()

            pe.wait_ge(tile_added, T0 + OPEN_BANKS)
            pe.wait_ge(hot_copied, T0 // GROUP + 2)
            pe.wait_ge(factors_made, T0 // GROUP + 1)
            pe.wait_ge(ld_bias_first, 16)
            for half in range(2):
                mine = range(half * HALF, (half + 1) * HALF)
                per = P // BN
                for w in mine:
                    m = min(P, (NB - per * w) * BN)
                    if w >= BANKS:
                        pe.wait_ge(x1_made, w - BANKS + 1)
                    first = mm(psum[0:m, w % BANKS, :], ones_row[:, 0:m], bias_row, start=True, stop=False)
                    if w == HALF:
                        first.then_inc(base_used, 1)
                for b in range(BASES):
                    for c in range(KC):
                        chunk = (half * BASES + b) * KC + c
                        pe.wait_ge(ld_base[chunk % 2], 16 * (chunk // 2 + 1))
                        end = b == BASES - 1 and c == KC - 1
                        for w in mine:
                            m = min(P, (NB - per * w) * BN)
                            last = mm(psum[0:m, w % BANKS, :], sums[:, c, per * w * P + b:(per * w + m // BN) * P:BASES],
                                      base_ring[:, chunk % 2, :], start=False, stop=end)
                            if end:
                                last.then_inc(layer0_done, 1)
                        if not end:
                            last.then_inc(base_used, 1)

            for layer in range(LAYERS):
                rows_in = h_n if layer == 0 else acc
                if layer:
                    pe.wait_ge(tile1_added, layer * T1 + OPEN_BANKS)
                for w in range(NW):
                    if layer == 0:
                        pe.wait_ge(normed, NW + w + 1)
                    if w >= 2:
                        pe.wait_ge(turned_sb, layer * NW + w - 1)
                    for c in range(KC):
                        last = nc.tensor.transpose(psum[:, 2 + w % 2, c * P:c * P + rows(w)],
                                                   rows_in[0:rows(w), w, c * P:(c + 1) * P], ident[0:rows(w), 0:rows(w)])
                    last.then_inc(turned, 1)
                pe.wait_ge(turned_sb, (layer + 1) * NW)
                if layer:
                    pe.wait_ge(root_in, layer * NW)
                for w in range(NW):
                    for c in range(KC):
                        last = mm(psum[0:rows(w), 7, RELS * w:RELS * (w + 1)], h_t[:, c, w * P:w * P + rows(w)],
                                  gates[:, layer, :, c], start=(c == 0), stop=(c == KC - 1))
                last.then_inc(gate_sum, 1)

                carry_from = 2
                if layer == 0:
                    count_totals(order1, 1)
                pe.wait_ge(ld_w[layer], 16 * (RELS + 1))
                done = 0
                for w in range(NW):
                    for r in range(RELS):
                        n = (layer * NW + w) * RELS + r
                        if w * RELS + r >= 4:
                            pe.wait_ge(product_sb, n - 3)
                        for c in range(KC):
                            last = mm(psum[0:rows(w), 2 + n % 4, :], h_t[:, c, w * P:w * P + rows(w)], w_sb[:, r, c, :],
                                      start=(c == 0), stop=(c == KC - 1))
                        last.then_inc(product, 1)
                    if layer:
                        continue
                    if w == 0:
                        count_tiles(order1, 1)
                    elif w == 1:
                        sum_slots(order1, 1)
                        sum_buckets(order1, 1)
                    elif w == 2:
                        pe.wait_ge(window_made, 1)
                        carry_open(range(2), order1)
                    while w >= 2 and done < min(CHUNKS, -(-CHUNKS * (w - 1) // (NW - 2))):
                        carry_chunk(sets1, [g_row, g_code], range(2), order1, done % 2, CHUNKS // 2 + done // 2 + 1)
                        done += 1
                if layer == 0:
                    carry_open(range(2), order1, stop=True).then_inc(carry_end, 1)

                pe.wait_ge(ld_bias[layer], 16)
                pe.wait_ge(gate_made, 2 * (layer + 1))
                for w in range(NW):
                    if w >= 2:
                        pe.wait_ge(root_in, layer * NW + w - 1)
                    mm(psum[0:rows(w), 6 + w % 2, :], ones_row[:, 0:rows(w)], bias_row, start=True, stop=False)
                    for c in range(KC):
                        last = mm(psum[0:rows(w), 6 + w % 2, :], h_t[:, c, w * P:w * P + rows(w)], root_sb[:, c, :],
                                  start=False, stop=(c == KC - 1))
                    last.then_inc(root_sum, 1)

                pe.wait_ge(slots1_made, 1)
                pe.wait_ge(product_sb, (layer + 1) * NW * RELS)
                with pe.Fori(0, T1 // FETCHES) as i:
                    for k in range(FETCHES):
                        pe.wait_ge(slot_hot_made, i * FETCHES + (layer * (T1 + OPEN_BANKS) + k + 1))
                        pe.wait_ge(fetched1[k % SLOTS1],
                                   i * (16 * FETCHES // SLOTS1) + 16 * (layer * T1 // SLOTS1 + k // SLOTS1 + 1))
                        pe.wait_ge(tile1_added, i * FETCHES + (layer * T1 + k + 1))
                        mm(psum[:, k % OPEN_BANKS, :], slot_hot[:, k % PE_TILES, :], ring1[:, k % SLOTS1, :],
                           start=True, stop=True).then_inc(tile1_done, 1)


_INS = ["x", "src", "dst", "edge_type_2", "edge_type_32", "edge_weight1", "L0_gnn_bases", "L0_gnn_w_comp",
        "L0_gnn_h_bias", "L1_gnn_basis1", "L1_gnn_att1", "L1_gnn_gate_w1", "L1_gnn_root1", "L1_gnn_bias1",
        "L1_gnn_basis2", "L1_gnn_att2", "L1_gnn_gate_w2", "L1_gnn_root2", "L1_gnn_bias2"]


def build(nc, a, out):
    gnn(nc, a["x"], a["src"], a["dst"], a["edge_type_2"], a["edge_type_32"], a["edge_weight1"], a["L0_gnn_bases"],
        a["L0_gnn_w_comp"], a["L0_gnn_h_bias"],
        *([a[f"L1_gnn_{name}{n}"] for n in (1, 2)] for name in ("basis", "att", "gate_w", "root", "bias")), out)


def kernel(**inputs):
    import numpy as np
    import concourse.bacc as bacc
    from concourse.bass_utils import run_bass_kernel_spmd

    nc = bacc.Bacc("TRN2", target_bir_lowering=False, num_devices=1)
    arrays = {f"in_{n}": np.ascontiguousarray(inputs[n]) for n in _INS}
    args = {n: nc.dram_tensor(f"in_{n}", arrays[f"in_{n}"].shape, mybir.dt.from_np(arrays[f"in_{n}"].dtype),
                              kind="ExternalInput").ap() for n in _INS}
    out = nc.dram_tensor("out", (N, D), F32, kind="ExternalOutput").ap()
    build(nc, args, out)
    return run_bass_kernel_spmd(nc, [arrays], core_ids=[0]).results[0]["out"]
```

```python
from contextlib import ExitStack

import concourse.bass as bass
from concourse import mybir

F32 = mybir.dt.float32
F16 = mybir.dt.float16
BF16 = mybir.dt.bfloat16
I32 = mybir.dt.int32
ALU = mybir.AluOpType
ACT = mybir.ActivationFunctionType

P = 128
N = 1250
D = 512
E = 20000
KC = D // P
NW = -(-N // P)
LAST = N - (NW - 1) * P
EP, ET = 125, 160
BASES = 8
TYPES = 32
RELS = 2
ATT = 30
LAYERS = 2
BN = P // BASES
NB = -(-N // BN)
GROUP = 4
AHEAD = 2 * GROUP
SLOTS = 8
SLOTS1 = 28
DVE_TILES = 24
PE_TILES = 8
FETCHES, IDX = 24, 12
FETCHES1, IDX1 = 56, 14
TC = 8
CHUNKS = ET // TC
PARTS = 5
PARTS1 = 2
BANKS = 8
BANK = 512
WRING = 3
OPEN_BANKS = 4
MIX_STEPS = 16
MIX_ROWS = 4 * MIX_STEPS
MIX_GROUPS = 6
MIX_EARLY = 4
MIX_LOAD = 4
MIX_PARTS = MIX_STEPS // MIX_LOAD
MRING = 4
X_AFTER = 10
MIX_CHUNKS = MIX_GROUPS * MIX_ROWS // P
MIX_HALF = (LAYERS * KC - MIX_CHUNKS) // 2 + 1
CARRY_FROM = 4
ROOTS_FIRST = (5, 4)
MIX_CUT = 7
ROOTS_AT = (NW - 2, NW - 1)
ROOT_EVERY = 5
HALF = NW // 2
EPS = 1e-5


def tiles_for(buckets, fetches):
    worst = (E + buckets * (P - 1)) // P
    return -(-worst // fetches) * fetches


T0 = tiles_for(NB, FETCHES)
T1 = tiles_for(NW, FETCHES1)
ds = bass.ds


def rows(w):
    return LAST if w == NW - 1 else P


class Space:

    def __init__(self, base, start=0, end=None):
        self.base, self.at, self.end = base, start, end if end is not None else base.shape[1]

    def words(self, n, parts=P, dt=F32):
        assert self.at + n <= self.end, (self.at, n, self.end)
        got = self.base[0:parts, self.at:self.at + n]
        self.at += n
        return got if dt == F32 else got.bitcast(dt)

    def halves(self, n, dt, parts=P):
        return self.words(-(-n // 2), parts, dt)[:, 0:n]


class Order:

    def __init__(self, nb, tiles, space, bank, bank_sums):
        self.nb, self.tiles = nb, tiles
        cube = nb * ET
        self.hot = space.halves(cube, F16, EP)
        self.count = space.halves(cube, F16, EP)
        self.base = space.halves(cube, F16, EP)
        self.key = space.halves(ET, F16, EP)
        self.slot_q = space.halves(ET, F16, EP)
        self.tile_grid = space.halves(tiles * TC, F16, EP).rearrange("p (q t) -> p q t", t=TC)
        self.slot_r = space.halves(ET, F16, EP)
        self.int_a = space.words(ET, EP, I32)
        self.int_b = space.words(ET, EP, I32)
        self.ends = space.words(nb + 1, EP)
        self.own = space.halves(nb, BF16, EP)
        self.nt_i = space.words(nb, EP, I32)
        self.nt = space.words(nb, EP)
        self.upto = space.words(nb, EP)
        self.low = space.halves(nb, F16, EP)
        self.high = space.halves(nb, F16, EP)
        self.before = space.words(nb, EP)
        self.col_i = space.words(1, nb, I32)
        self.col_nt = space.halves(1, BF16, nb)
        self.col_end = space.words(1, nb)
        self.past = space.halves(tiles, BF16, nb)
        self.p_before = bank[0:EP, 0:nb]
        self.p_total = bank[0:EP, P:P + nb]
        self.p_down = bank[0:nb, 2 * P - 2:2 * P - 1]
        self.p_end = bank[0:nb, 2 * P - 1:2 * P]
        self.p_bucket = bank[0:1, 2 * P:2 * P + tiles]
        self.p_low = bank_sums[0:EP, 0:ET]
        self.p_high = bank_sums[0:EP, ET:2 * ET]


def part_of(words, field):
    return words.bitcast(field.dtype).rearrange("p (r t) -> p r t", t=TC)


def by_bucket(ap, nb):
    return ap.rearrange("p (k t) -> p k t", k=nb)


def gnn(nc, x, src, dst, edge_type_2, edge_type_32, edge_weight1, bases0, w_comp, h_bias,
        basis, att, gate_w, root, bias, out):
    with ExitStack() as ctx:
        def sb(name, shape, dt=F32):
            return ctx.enter_context(nc.sbuf_tensor(name, shape, dt))

        def sem(name):
            return ctx.enter_context(nc.semaphore(name))

        psum = ctx.enter_context(nc.psum_tensor("psum", [P, BANKS, BANK], F32))

        arena = sb("arena", [P, NB * D])
        region_x = sb("region_x", [P, NW * D])
        region_w = sb("region_w", [P, 4096])

        ident = sb("ident", [P, P])
        ident_b = sb("ident_b", [P, P], BF16)
        before_b = sb("before_b", [P, P], BF16)
        ones_b = sb("ones_b", [P, P], BF16)
        zeros_b = sb("zeros_b", [P, P], BF16)
        count1 = sb("count1", [P, P])
        count_t = sb("count_t", [P, T0], F16)
        ones_row = sb("ones_row", [1, P])
        att_row = sb("att_row", [1, LAYERS * RELS * ATT])
        att_all = sb("att_all", [P, LAYERS * RELS * ATT])
        row_grid = sb("row_grid", [P, P * TC], F16)
        comp = sb("comp", [P, GROUP * BASES])
        comp_rest = sb("comp_rest", [P, GROUP * BASES])
        comp_part = [sb(f"comp_part{i}", [P, GROUP * BASES], BF16) for i in range(3)]
        stats = sb("stats", [P, NW, 6])
        moments = sb("moments", [P, NW, 2])
        scale = sb("scale", [P, NW])
        shift = sb("shift", [P, NW])
        source = sb("source", [P, T0 + IDX], I32)
        place = sb("place", [P, T0 + AHEAD])
        kind = sb("kind", [P, T0 + AHEAD])
        weight = sb("weight", [P, T0 + AHEAD])
        bucket = sb("bucket", [1, T0], I32)
        index_slots = sb("index_slots", [P, FETCHES1], I32)
        kind_hot = sb("kind_hot", [P, GROUP, TYPES], BF16)
        kind_hot_t = sb("kind_hot_t", [P, P], BF16)
        place_hot = sb("place_hot", [P, GROUP, BN])
        factor = sb("factor", [P, GROUP, BASES])

        x_sb = region_x[:].rearrange("p (w d) -> p w d", d=D)
        rx = Space(region_x)
        ring0 = rx.words(SLOTS * D).rearrange("p (s d) -> p s d", d=D)
        factors = rx.words(2 * GROUP * P).rearrange("p (g j c) -> p g j c", g=2, j=GROUP)

        def carrying_set(space, parts, tiles):
            return (space.halves(P * TC, F16, EP).rearrange("p (r t) -> p r t", t=TC),
                    [space.words(P * TC // 2, EP) for _ in range(parts)],
                    space.halves(TC * tiles, BF16, EP).rearrange("p (q t) -> p q t", t=TC))

        rx = Space(region_x)
        sets0 = [carrying_set(rx, PARTS, T0), carrying_set(Space(region_w), PARTS, T0)]

        a0 = Space(arena)
        h_out = a0.words(NW * D).rearrange("p (w d) -> p w d", d=D)
        early = a0.at + 3 * NB * ET // 2
        order0 = Order(NB, T0, a0, psum[:, 0, :], psum[:, 1, :])
        e_dst, e_src, e_kind = (a0.words(ET, EP, I32) for _ in range(3))
        e_weight, e_rest, e_place = (a0.words(ET, EP) for _ in range(3))
        e_last = a0.words(ET, EP)
        e_int = a0.words(ET, EP, I32)
        f_source, f_code = a0.halves(ET, F16, EP), a0.halves(ET, F16, EP)
        f_weight = [a0.halves(ET, BF16, EP) for _ in range(3)]
        s_int = a0.words(T0, P, I32)
        s_int_b = a0.words(T0, P, I32)
        mix_at = a0.at
        mix_load = a0.words(MRING * MIX_LOAD * D, 4 * ATT).rearrange("p (g s d) -> p g s d", g=MRING, s=MIX_LOAD)
        mix_out = a0.words(2 * D).rearrange("p (g d) -> p g d", g=2)
        mix_att = a0.words(MIX_STEPS - 1 + P, 4 * ATT)
        used = a0.at

        sums = arena[:].rearrange("p (c m) -> p c m", c=KC)

        rw = Space(region_w)
        base_ring = rw.words(2 * D).rearrange("p (s d) -> p s d", s=2)
        basis_ring = rw.words(WRING * D).rearrange("p (s d) -> p s d", s=WRING)
        mix = rw.words(RELS * D).rearrange("p (r d) -> p r d", r=RELS)
        bias_all = rw.words(D)

        cut, width = HALF * (P // BN) * P, NB * P
        free1 = [Space(arena, c * width, c * width + cut) for c in range(KC)]
        free2 = [Space(arena, c * width + cut, (c + 1) * width) for c in range(KC)]
        h_n = free1[0].words(NW * D).rearrange("p (w d) -> p w d", d=D)
        w_sb = free1[1].words(RELS * KC * D).rearrange("p (r c d) -> p r c d", r=RELS, c=KC)
        slot_hot_flat = free1[1].words(PE_TILES * P)
        slot_hot = slot_hot_flat.rearrange("p (s m) -> p s m", s=PE_TILES)
        gate_all = slot_hot_flat[:, 0:D]
        h_t = free1[2].words(KC * NW * P).rearrange("p (c n) -> p c n", c=KC)
        root_sb = free1[3].words(KC * D).rearrange("p (c d) -> p c d", c=KC)
        gates = free1[3].words(LAYERS * RELS * D).rearrange("p (l r d) -> p l r d", l=LAYERS, r=RELS)
        gate = free1[3].words(RELS * NW).rearrange("p (w r) -> p w r", r=RELS)
        gate_in = free1[3].words(RELS * NW).rearrange("p (w r) -> p w r", r=RELS)
        row_of = free1[3].words(T1 + IDX1, P, I32)
        minus_local = free1[3].words(T1)
        off = free1[3].words(2 * P).rearrange("p (s m) -> p s m", s=2)
        window = free1[3].words(T1, 1, I32)
        acc_flat = Space(arena, KC * width - NW * D).words(NW * D)
        assert free1[3].at <= KC * width - NW * D
        acc = acc_flat.rearrange("p (w d) -> p w d", d=D)
        rw = Space(region_w, 0, 4096 - D)
        gated = rw.words(2 * RELS * D).rearrange("p (b r d) -> p b r d", b=2, r=RELS)
        a2, a3 = Space(arena, free2[0].at, free2[0].end), Space(arena, free2[1].at, free2[1].end)
        order1 = Order(NW, T1, a2, psum[:, 0, :], psum[:, 1, :])
        g_dst, g_src, g_rel = (a3.words(ET, EP, I32) for _ in range(3))
        g_place = a3.words(ET, EP)
        g_row, g_code = a3.halves(ET, F16, EP), a3.halves(ET, F16, EP)
        a4 = Space(arena, free2[2].at, free2[2].end)
        sets1 = [carrying_set(space, PARTS1, T1) for space in (a4, a3)]
        t_int = a4.words(T1, P, I32)
        t_int_b = a4.words(T1, P, I32)
        t_f = a4.words(T1)
        ring1 = [space.words(D) for space in (*free2[:3], rw) for _ in range((space.end - space.at) // D)][:SLOTS1]
        assert len(ring1) == SLOTS1

        h_table = nc.dram_tensor("h_table", [N, D], F32).ap()
        gated_table = nc.dram_tensor("gated_table", [RELS * N, D], F32).ap()
        w_table = nc.dram_tensor("w_table", [LAYERS, RELS, D, D], F32).ap()

        ld_edges, ld_x, ld_small, ld_x2 = sem("ld_edges"), sem("ld_x"), sem("ld_small"), sem("ld_x2")
        ld_gates = sem("ld_gates")
        ld_edges1, ld_bias, ld_acc = sem("ld_edges1"), sem("ld_bias"), sem("ld_acc")
        ld_bias_first = sem("ld_bias_first")
        ld_base = [sem(f"ld_base{i}") for i in range(2)]
        ld_basis = [sem(f"ld_basis{i}") for i in range(WRING)]
        ld_w = [sem(f"ld_w{i}") for i in range(LAYERS)]
        st_h, st_mix = sem("st_h"), sem("st_mix")
        st_gated = [sem(f"st_gated{i}") for i in range(2)]
        st_out = sem("st_out")
        fetched = [sem(f"fetched{i}") for i in range(SLOTS)]
        fetched1 = [sem(f"fetched1_{i}") for i in range(SLOTS1)]
        ld_att, ld_mix = sem("ld_att"), [sem(f"ld_mix{i}") for i in range(MRING)]
        st_first = [sem(f"st_first{i}") for i in range(2)]
        mix_read = sem("mix_read")
        mix_copied = sem("mix_copied")
        consts = sem("consts")
        numbers = sem("numbers")
        cleared = sem("cleared")
        dve = sem("dve")
        prepared = sem("prepared")
        zeroed = sem("zeroed")
        counted = sem("counted")
        total = sem("total")
        tiles_down = sem("tiles_down")
        ends_down = sem("ends_down")
        past_made = sem("past_made")
        bucket_sum = sem("bucket_sum")
        split = sem("split")
        slot_sum = sem("slot_sum")
        carry_made = [sem(f"carry_made{i}") for i in range(2)]
        carried = [sem(f"carried{i}") for i in range(2)]
        last_made = [sem(f"last_made{i}") for i in range(2)]
        act_step = sem("act_step")
        row_hot_made = sem("row_hot_made")
        slots_known = sem("slots_known")
        att_spread = sem("att_spread")
        factor_step = sem("factor_step")
        carry_end = sem("carry_end")
        x_stats, x_scaled = sem("x_stats"), sem("x_scaled")
        rooted = sem("rooted")
        normed = sem("normed")
        window_made = sem("window_made")
        slots_made = sem("slots_made")
        hot_made = sem("hot_made")
        hot_turned = sem("hot_turned")
        hot_copied = sem("hot_copied")
        looked_up = sem("looked_up")
        factors_made = sem("factors_made")
        index_copied = sem("index_copied")
        pool_step = sem("pool_step")
        tile_done = sem("tile_done")
        tile_added = sem("tile_added")
        base_used = sem("base_used")
        layer0_done = sem("layer0_done")
        mixed = sem("mixed")
        x1_made = sem("x1_made")
        turned = sem("turned")
        turned_sb = sem("turned_sb")
        gate_sum = sem("gate_sum")
        gate_made = sem("gate_made")
        product = sem("product")
        product_sb = sem("product_sb")
        root_sum = sem("root_sum")
        bias_added = sem("bias_added")
        root_in = sem("root_in")
        slots1_made = sem("slots1_made")
        distance = sem("distance")
        slot_hot_made = sem("slot_hot_made")
        tile1_done = sem("tile1_done")
        tile1_added = sem("tile1_added")
        index1_copied = sem("index1_copied")

        block = ctx.enter_context(nc.Block())

        def windows(dram, sbuf, engine, to_dram, signal):
            full, rest = dram[0:(NW - 1) * P, :].rearrange("(w p) d -> p w d", p=P), dram[(NW - 1) * P:N, :]
            for a, b in ((full, sbuf[:, 0:NW - 1, :]), (rest, sbuf[0:LAST, NW - 1, :])):
                engine.dma_start(a if to_dram else b, b if to_dram else a).then_inc(signal, 16)

        mix_left = [(layer, c) for layer in range(LAYERS) for c in range(KC)][MIX_CHUNKS:]
        turn_bank = psum[:, 4, 0:P // 2].bitcast(BF16)
        edge_table = lambda a: a.rearrange("(p t) -> p t", p=EP)

        @block.sync
        def _(sp):
            sp.dma_start(e_dst, edge_table(dst)).then_inc(ld_edges, 16)
            sp.dma_start(e_src, edge_table(src)).then_inc(ld_edges, 16)
            sp.dma_start(e_kind, edge_table(edge_type_32)).then_inc(ld_edges, 16)
            sp.dma_start(e_weight, edge_weight1.rearrange("(p t) o -> p (t o)", p=EP)).then_inc(ld_edges, 16)
            def load_mixing(n):
                sp.wait_ge(mix_read, n + 1)
                for q in range(4):
                    row = n // MIX_PARTS * MIX_ROWS + q * MIX_STEPS + n % MIX_PARTS * MIX_LOAD
                    sp.dma_start(mix_load[q * ATT:(q + 1) * ATT, n % MRING], basis[0][:, row:row + MIX_LOAD, :]
                                 ).then_inc(ld_mix[n % MRING], 16)

            load_mixing(0)
            sp.wait_ge(zeroed, 1)
            for r in range(RELS):
                for q in range(4):
                    at = MIX_STEPS - 1 + r * MIX_ROWS + q * MIX_STEPS
                    sp.dma_start(mix_att[q * ATT:(q + 1) * ATT, at:at + 1],
                                 att[0][r:r + 1, :].rearrange("r b -> b r")).then_inc(ld_att, 16)
            for n in range(1, MIX_GROUPS * MIX_PARTS):
                if n == X_AFTER:
                    windows(x, x_sb, sp, False, ld_x)
                load_mixing(n)
            for j in range(GROUP):
                sp.dma_start(comp[TYPES * j:TYPES * (j + 1), BASES * j:BASES * (j + 1)], w_comp).then_inc(ld_small, 16)
            for layer in range(LAYERS):
                n = RELS * ATT
                sp.dma_start(att_row[0:1, layer * n:(layer + 1) * n],
                             att[layer].rearrange("(a r) b -> a (r b)", a=1)).then_inc(ld_small, 16)
            sp.wait_ge(normed, NW)
            windows(h_table, h_out, sp, True, st_h)

            sp.wait_ge(carry_end, 1)
            sp.dma_start(bias_all, h_bias.rearrange("(a d) -> a d", a=1).broadcast_to((P, D))).then_inc(ld_bias_first, 16)

            def load_bases(half, b, chunks=range(KC)):
                for c in chunks:
                    sp.wait_ge(base_used, b * KC + (half * BASES * KC + c + 1))
                    sp.dma_start(base_ring[:, c % 2, :],
                                 bases0[ds(b, 1), c * P:(c + 1) * P, :].rearrange("b i o -> i (b o)")
                                 ).then_inc(ld_base[c % 2], 16)

            def load_weights(layer, piece):
                to, of = (w_sb[:, piece], w_table[layer, piece]) if piece < RELS else (root_sb, root[layer])
                sp.dma_start(to, of.rearrange("(c p) o -> p c o", p=P)).then_inc(ld_w[layer], 16)

            load_bases(0, 0, range(2))
            sp.wait_ge(tile_added, 4 + T0)
            sp.wait_ge(factors_made, T0 // GROUP + 1)
            load_bases(0, 0, range(2, KC))
            for w in range(0, NW, 2):
                load_bases(0, 1 + w // 2)
                for at in (w, w + 1):
                    sp.dma_start(x_sb[0:rows(at), at, :], x[at * P:at * P + rows(at), :]).then_inc(ld_x2, 16)
            with sp.Fori(1 + NW // 2, BASES) as b:
                load_bases(0, b)
            load_bases(1, 0)
            sp.wait_ge(layer0_done, HALF)
            for l in range(LAYERS):
                for r in range(RELS):
                    sp.dma_start(gates[:, l, r, :], gate_w[l][r:r + 1].rearrange("r i o -> r (i o)").broadcast_to((P, D))
                                 ).then_inc(ld_gates, 16)
            sp.wait_ge(st_mix, 16 * (KC - MIX_CHUNKS))
            for i in range(2):
                sp.wait_ge(st_first[i], 16 * RELS * MIX_GROUPS // 2)
            for piece in range(RELS + 1):
                load_bases(1, 1 + piece)
                load_weights(0, piece)
            with sp.Fori(RELS + 2, BASES) as b:
                load_bases(1, b)

            for layer in range(LAYERS):
                if layer == 0:
                    sp.wait_ge(layer0_done, NW)
                    for dram, sbuf in ((dst, g_dst), (src, g_src), (edge_type_2, g_rel)):
                        sp.dma_start(sbuf, edge_table(dram)).then_inc(ld_edges1, 16)
                    for w in range(NW):
                        sp.dma_start(acc[:, w, :], bias[0].rearrange("(a d) -> a d", a=1).broadcast_to((P, D))
                                     ).then_inc(ld_acc, 16)
                    sp.dma_start(bias_all, bias[1].rearrange("(a d) -> a d", a=1).broadcast_to((P, D))
                                 ).then_inc(ld_bias, 16)
                else:
                    sp.wait_ge(root_sum, NW)
                    sp.wait_ge(st_mix, 16 * (LAYERS * KC - MIX_CHUNKS))
                    for piece in range(RELS + 1):
                        load_weights(1, piece)
                if layer == 1:
                    sp.wait_ge(tile1_done, SLOTS1 + T1)
                for w in range(NW):
                    for r in range(RELS):
                        sp.wait_ge(product_sb, (layer * NW + w) * RELS + r + 1)
                        sp.dma_start(gated_table[r * N + w * P:r * N + w * P + rows(w), :],
                                     gated[0:rows(w), w % 2, r, :]).then_inc(st_gated[w % 2], 16)

            sp.wait_ge(tile1_added, LAYERS * T1 + OPEN_BANKS)
            windows(out, x_sb, sp, True, st_out)
            sp.wait_ge(st_out, 32)

        @block.gpsimd
        def _(pool):
            pool.iota(count1[:], [[1, P]], base=1, channel_multiplier=0,
                      allow_small_or_imprecise_dtypes=True).then_inc(consts, 1)
            pool.iota(count_t[:], [[1, T0]], base=0, channel_multiplier=0,
                      allow_small_or_imprecise_dtypes=True).then_inc(consts, 1)
            pool.iota(row_grid[:].rearrange("p (r t) -> p r t", t=TC), [[1, P], [0, TC]], base=0, channel_multiplier=0,
                      allow_small_or_imprecise_dtypes=True).then_inc(consts, 1)
            def tile_numbers(order, made):
                pool.iota(order.tile_grid, [[1, order.tiles], [0, TC]], base=0, channel_multiplier=0,
                          allow_small_or_imprecise_dtypes=True).then_inc(made, 1)

            pool.memset(ident[:], 0.0).then_inc(pool_step, 1)
            pool.memset(before_b[:], 1.0).then_inc(pool_step, 1)
            pool.wait_ge(pool_step, 2)
            pool.affine_select(out=ident[:], in_=ident[:], compare_op=ALU.not_equal, fill=1.0, base=0,
                               pattern=[[-1, P]], channel_multiplier=1).then_inc(consts, 1)
            pool.affine_select(out=before_b[:], in_=before_b[:], compare_op=ALU.is_gt, fill=0.0, base=0,
                               pattern=[[1, P]], channel_multiplier=-1).then_inc(consts, 1)

            tile_numbers(order0, numbers)

            pool.memset(arena[:, used:], 0.0).then_inc(cleared, 1)
            pool.wait_ge(slots_known, 1)
            pool.wait_ge(st_h, 32)
            pool.memset(arena[:, 0:early], 0.0).then_inc(cleared, 1)
            for i in range(2):
                pool.wait_ge(st_first[i], 16 * RELS * MIX_GROUPS // 2)
            pool.memset(arena[:, mix_at:used], 0.0).then_inc(cleared, 1)
            pool.wait_ge(slots_made, 1)
            pool.memset(arena[:, early:mix_at], 0.0).then_inc(cleared, 1)

            def fetch(table, index, slots, ring, done, freed, tiles, copied, base, fetches, idx):
                part = lambda h: index_slots[:, h * idx:(h + 1) * idx]
                parts = fetches // idx
                copies = base // tiles * (parts * tiles // fetches + 1)
                if copies:
                    pool.wait_ge(copied, copies)
                pool.tensor_copy(part(0), index[:, 0:idx]).then_inc(copied, 1)
                with pool.Fori(0, tiles // fetches) as i:
                    for k in range(fetches):
                        if k % 2 == 0:
                            pool.wait_ge(freed, i * fetches + (base + k + 2))
                            pool.sem_inc(pool_step, 1)
                        if k % idx == idx - 2:
                            pool.tensor_copy(part((k // idx + 1) % parts),
                                             index[:, ds(i * fetches + (k // idx + 1) * idx, idx)]).then_inc(copied, 1)
                        if k % idx == 0:
                            pool.wait_ge(copied, i * parts + (k // idx + 1 + copies))
                            pool.sem_inc(pool_step, 1)
                        pool.indirect_dma_start(ring[k % slots], None, table,
                                                bass.IndirectOffsetOnAxis(index_slots[:, k:k + 1], 0)
                                                ).then_inc(done[k % slots], 16)

            fetch(h_table, source, SLOTS, [ring0[:, k, :] for k in range(SLOTS)], fetched, tile_done, T0, index_copied, 0, FETCHES, IDX)

            pool.wait_ge(layer0_done, NW)
            tile_numbers(order1, numbers)
            pool.wait_ge(index_copied, 2 * T0 // FETCHES + 1)
            pool.wait_ge(slots1_made, 1)
            for layer in range(LAYERS):
                for half in range(2):
                    pool.wait_ge(st_gated[half], 16 * (layer + 1) * RELS * (NW // 2))
                fetch(gated_table, row_of, SLOTS1, ring1, fetched1, tile1_done, T1, index1_copied, layer * T1,
                      FETCHES1, IDX1)

        @block.scalar
        def _(act):
            def store_mixed(groups):
                for g in groups:
                    act.wait_ge(mix_read, MRING + (g + 1) * MIX_PARTS)
                    if g >= 2:
                        act.wait_ge(st_first[g % 2], 16 * RELS * (g // 2))
                    nc.scalar.copy(mix_out[:, g % 2, :], psum[:, 7, :]).then_inc(mix_copied, 1)
                    act.wait_ge(mix_copied, g + 1)
                    for r in range(RELS):
                        act.dma_start(w_table[0, r, g * MIX_ROWS:(g + 1) * MIX_ROWS, :],
                                      mix_out[r * MIX_ROWS:(r + 1) * MIX_ROWS, g % 2, :]).then_inc(st_first[g % 2], 16)

            store_mixed(range(MIX_EARLY))
            act.wait_ge(x_stats, 1)
            nc.scalar.activation(scale[:], moments[:, :, 1], ACT.Sqrt).then_inc(rooted, 1)
            act.wait_ge(x_scaled, 1)
            for w in range(NW):
                nc.scalar.activation(h_out[:, w, :], x_sb[:, w, :], ACT.Relu, bias=shift[:, w:w + 1],
                                     scale=scale[:, w:w + 1]).then_inc(normed, 1)

            store_mixed(range(MIX_EARLY, MIX_GROUPS))
            with act.Fori(0, CHUNKS // 2) as i:
                for k in range(2):
                    row_hot, row_parts, _ = sets0[k]
                    act.wait_ge(row_hot_made, i * 2 + (k + 1))
                    act.sem_inc(act_step, 1)
                    for t in range(TC):
                        last = nc.scalar.activation(part_of(row_parts[-1], f_weight[-1])[:, :, t], row_hot[:, :, t], ACT.Copy,
                                                    scale=e_last[:, ds((i * 2 + k) * TC + t, 1)])
                    last.then_inc(last_made[k], 1)

            act.wait_ge(hot_turned, 1)
            nc.scalar.copy(kind_hot_t[:], turn_bank).then_inc(hot_copied, 1)
            with act.Fori(0, T0 // GROUP + 1) as g:
                act.wait_ge(looked_up, g + 1)
                act.wait_ge(hot_turned, g + 2)
                nc.scalar.activation(kind_hot_t[:], turn_bank, ACT.Copy).then_inc(hot_copied, 1)

            def stream_bases(chunks):
                for layer, c in chunks:
                    block_at = layer * KC + c - MIX_CHUNKS
                    with act.Fori(0, ATT // WRING) as j:
                        for s in range(WRING):
                            act.wait_ge(mixed, j * (2 * WRING) + (block_at * ATT + s + 1) * RELS)
                            act.dma_start(basis_ring[:, s, :],
                                          basis[layer][ds(j * WRING + s, 1), c * P:(c + 1) * P, :].rearrange("b i o -> i (b o)")
                                          ).then_inc(ld_basis[s], 16)
                    act.wait_ge(mixed, 2 * WRING + (block_at + 1) * ATT * RELS)
                    act.dma_start(w_table[layer, :, c * P:(c + 1) * P, :].rearrange("r i o -> i r o"),
                                  mix).then_inc(st_mix, 16)

            def norm_half(half):
                mine = slice(half * HALF, (half + 1) * HALF)
                act.wait_ge(x_stats, half + 2)
                nc.scalar.activation(scale[:, mine], moments[:, mine, 1], ACT.Sqrt).then_inc(rooted, 1)
                act.wait_ge(x_scaled, half + 2)
                for w in range(NW)[mine]:
                    nc.scalar.activation(h_n[0:rows(w), w, :], x_sb[0:rows(w), w, :], ACT.Relu,
                                         bias=shift[0:rows(w), w:w + 1], scale=scale[0:rows(w), w:w + 1]).then_inc(normed, 1)

            stream_bases(mix_left[:MIX_HALF])
            norm_half(0)
            stream_bases(mix_left[MIX_HALF:])
            act.wait_ge(st_mix, 16 * len(mix_left))

            for layer in range(LAYERS):
                for w in range(NW + 1):
                    if w < NW:
                        act.wait_ge(turned, layer * NW + w + 1)
                        nc.scalar.activation(h_t[:, :, w * P:w * P + rows(w)],
                                             psum[:, 2 + w % 2, :].rearrange("p (c n) -> p c n", c=KC)[:, :, 0:rows(w)],
                                             ACT.Relu).then_inc(turned_sb, 1)
                    if w == 0:
                        continue
                    if w == 2 and layer == 0:
                        norm_half(1)
                    done = w - 1
                    n = layer * NW + done
                    act.wait_ge(gate_sum, (n + 1) * RELS)
                    nc.scalar.activation(gate[0:rows(done), done, :], gate_in[0:rows(done), done, :],
                                         ACT.Sigmoid).then_inc(gate_made, 1)
                    act.wait_ge(gate_made, n + 1)
                    for r in range(RELS):
                        act.wait_ge(product, n * RELS + r + 1)
                        if r == 0 and n >= 2:
                            act.wait_ge(st_gated[n % 2], 16 * RELS * (n // 2))
                        nc.scalar.activation(gated[0:rows(done), done % 2, r, :],
                                             psum[0:rows(done), 4 + (n * RELS + r) % 4, :], ACT.Copy,
                                             scale=gate[0:rows(done), done, r:r + 1]).then_inc(product_sb, 1)
                act.wait_ge(slots1_made, 1)
                act.wait_ge(gate_sum, (layer + 1) * NW * RELS)
                with act.Fori(0, T1 // PE_TILES) as i:
                    for k in range(PE_TILES):
                        act.wait_ge(tile1_done, i * PE_TILES + (layer * T1 + k + 1 + SLOTS1 - PE_TILES))
                        act.sem_inc(act_step, 1)
                        nc.scalar.activation(off[:, k % 2, :], count1[:], ACT.Square,
                                             bias=minus_local[:, ds(i * PE_TILES + k, 1)]).then_inc(distance, 1)
                        act.wait_ge(distance, i * PE_TILES + (layer * T1 + k + 1))
                        nc.scalar.activation(slot_hot[:, k, :], off[:, k % 2, :], ACT.Relu, bias=1.0, scale=-1.0
                                             ).then_inc(slot_hot_made, 1)

        @block.vector
        def _(eng):
            v = nc.vector
            steps = {}

            def chain(ins, signal=dve):
                steps[signal.name] = steps.get(signal.name, 0) + 1
                ins.then_inc(signal, 1)
                eng.wait_ge(signal, steps[signal.name])

            def count_edges(o):
                hot, count = (by_bucket(a, o.nb) for a in (o.hot, o.count))
                over = lambda a: a.unsqueeze(2).broadcast_to((EP, o.nb, ET))
                chain(v.tensor_tensor(hot, o.key.unsqueeze(1).broadcast_to((EP, o.nb, ET)), over(count_t[0:EP, 0:o.nb]),
                                      ALU.is_equal))
                chain(v.tensor_tensor_scan(o.count, o.hot, o.hot, 0.0, ALU.add, ALU.max))
                chain(v.memset(o.ends[:, 0:1], 0.0))
                chain(v.tensor_copy(o.ends[:, 1:o.nb + 1], count[:, :, ET - 1]))
                chain(v.tensor_tensor(o.own, o.ends[:, 1:o.nb + 1], o.ends[:, 0:o.nb], ALU.subtract), counted)

            def place_edges(o, n):
                hot, count, base = (by_bucket(a, o.nb) for a in (o.hot, o.count, o.base))
                over = lambda a: a.unsqueeze(2).broadcast_to((EP, o.nb, ET))
                eng.wait_ge(total, n + 1)
                chain(v.tensor_scalar(o.col_i, o.p_down, float(P - 1), None, ALU.add))
                chain(v.tensor_scalar(o.nt_i, o.p_total, float(P - 1), None, ALU.add))
                chain(v.tensor_scalar(o.col_i, o.col_i, 7, None, ALU.arith_shift_right))
                chain(v.tensor_scalar(o.nt_i, o.nt_i, 7, None, ALU.arith_shift_right))
                chain(v.tensor_copy(o.nt, o.nt_i))
                chain(v.tensor_copy(o.before, o.p_before))
                chain(v.tensor_copy(o.col_nt, o.col_i), tiles_down)
                chain(v.tensor_tensor_scan(o.upto, o.nt, o.nt, 0.0, ALU.add, ALU.max))
                chain(v.tensor_tensor(o.upto, o.upto, o.nt, ALU.subtract))
                chain(v.scalar_tensor_tensor(o.upto, o.upto, float(P), o.before, ALU.mult, ALU.add))
                chain(v.tensor_tensor(o.upto, o.upto, o.ends[:, 0:o.nb], ALU.subtract))
                chain(v.tensor_copy(o.nt_i, o.upto))
                chain(v.tensor_scalar(o.nt_i, o.nt_i, P - 1, None, ALU.bitwise_and))
                chain(v.tensor_copy(o.low, o.nt_i))
                chain(v.tensor_copy(o.nt_i, o.upto))
                chain(v.tensor_scalar(o.nt_i, o.nt_i, 7, None, ALU.arith_shift_right))
                chain(v.tensor_copy(o.high, o.nt_i))
                chain(v.tensor_tensor(count, count, over(o.low), ALU.add))
                chain(v.tensor_tensor(o.count, o.count, o.hot, ALU.mult))
                chain(v.tensor_tensor(base, hot, over(o.high), ALU.mult), split)
                eng.wait_ge(ends_down, n + 1)
                chain(v.tensor_copy(o.col_end, o.p_end))
                chain(v.tensor_scalar(o.past, count_t[0:o.nb, 0:o.tiles], o.col_end, None, ALU.is_ge), past_made)

            def slots_of_edges(o, n):
                eng.wait_ge(slot_sum, n + 1)
                chain(v.tensor_scalar(o.int_a, o.p_low, 1.0, None, ALU.subtract))
                chain(v.tensor_scalar(o.int_b, o.int_a, P - 1, None, ALU.bitwise_and))
                chain(v.tensor_copy(o.slot_r, o.int_b))
                chain(v.tensor_scalar(o.int_a, o.int_a, 7, None, ALU.arith_shift_right))
                chain(v.tensor_tensor(o.slot_q, o.p_high, o.int_a, ALU.add), slots_known)

            def carry_edges(o, sets, fields, n, by_dve):
                grid = row_grid[0:EP, :].rearrange("p (r t) -> p r t", t=TC)
                eng.wait_ge(numbers, n + 1)
                with eng.Fori(0, CHUNKS // 2) as i:
                    for k in range(2):
                        row_hot, row_parts, tile_hot = sets[k]
                        col = (i * 2 + k) * TC
                        eng.wait_ge(carried[k], i + (n * (CHUNKS // 2) + 1))
                        v.tensor_tensor(row_hot, grid, o.slot_r[:, ds(col, TC)].unsqueeze(1).broadcast_to((EP, P, TC)),
                                        ALU.is_equal).then_inc(row_hot_made, 1)
                        v.tensor_tensor(tile_hot, o.tile_grid,
                                        o.slot_q[:, ds(col, TC)].unsqueeze(1).broadcast_to((EP, o.tiles, TC)), ALU.is_equal)
                        eng.wait_ge(row_hot_made, i * 2 + (k + 1 + n * CHUNKS))
                        for part, field in zip(row_parts, fields[:by_dve]):
                            last = v.tensor_tensor(part_of(part, field), row_hot,
                                                   field[:, ds(col, TC)].unsqueeze(1).broadcast_to((EP, P, TC)), ALU.mult)
                        last.then_inc(carry_made[k], 1)

            def norm_statistics(of, limit):
                for w in of:
                    last = v.bn_stats(stats[0:limit(w), w, :], x_sb[0:limit(w), w, :])
                chain(last)
                for w in of:
                    last = v.bn_aggr(moments[0:limit(w), w, :], stats[0:limit(w), w, :])
                chain(last)
                var = moments[:, of[0]:of[-1] + 1, 1]
                chain(v.tensor_scalar(var, var, EPS, None, ALU.add), x_stats)

            def norm_scales(of, n):
                mine = slice(of[0], of[-1] + 1)
                eng.wait_ge(rooted, n)
                chain(v.reciprocal(scale[:, mine], scale[:, mine]))
                chain(v.scalar_tensor_tensor(shift[:, mine], moments[:, mine, 0], -1.0, scale[:, mine], ALU.mult, ALU.mult),
                      x_scaled)

            def gate_sums(layer, of, source_rows):
                for w in of:
                    for r in range(RELS):
                        chain(v.scalar_tensor_tensor(gate_all[0:rows(w), :], source_rows[0:rows(w), w, :], 0.0,
                                                     gates[0:rows(w), layer, r, :], ALU.max, ALU.mult,
                                                     accum_out=gate_in[0:rows(w), w, r:r + 1]), gate_sum)

            v.memset(comp[:], 0.0)
            v.memset(mix_att, 0.0)
            v.memset(x_sb[:, NW - 1, :], 0.0).then_inc(zeroed, 1)
            v.memset(ones_b[:], 1.0)
            v.memset(zeros_b[:], 0.0)
            v.memset(ones_row[:], 1.0)
            v.memset(source[:], 0)
            for a in (place, kind, weight):
                v.memset(a[:], 0.0)
            eng.sem_inc(tile_added, OPEN_BANKS)
            eng.sem_inc(tile1_added, OPEN_BANKS)
            eng.sem_inc(mixed, 2 * WRING)
            eng.wait_ge(consts, 5)
            chain(v.tensor_copy(ident_b[:], ident[:]), prepared)

            eng.wait_ge(ld_edges, 64)
            chain(v.tensor_scalar(e_int, e_dst, 4, None, ALU.arith_shift_right))
            chain(v.tensor_copy(order0.key, e_int))
            count_edges(order0)
            place_edges(order0, 0)
            chain(v.tensor_copy(f_source, e_src))
            chain(v.tensor_scalar(e_int, e_dst, BN - 1, None, ALU.bitwise_and))
            chain(v.tensor_scalar(e_place, e_int, float(TYPES), None, ALU.mult))
            chain(v.tensor_tensor(f_code, e_place, e_kind, ALU.add))
            chain(v.tensor_copy(f_weight[0], e_weight))
            chain(v.tensor_tensor(e_rest, e_weight, f_weight[0], ALU.subtract))
            chain(v.tensor_copy(f_weight[1], e_rest))
            chain(v.tensor_tensor(e_rest, e_rest, f_weight[1], ALU.subtract))
            chain(v.tensor_copy(f_weight[2], e_rest))
            v.tensor_copy(e_last, f_weight[2])
            eng.wait_ge(ld_x, 32)
            norm_statistics(range(NW), lambda w: P)
            slots_of_edges(order0, 0)
            norm_scales(range(NW), 1)
            eng.wait_ge(normed, NW)
            carry_edges(order0, sets0, [f_source, f_code, *f_weight], 0, PARTS - 1)
            eng.wait_ge(ld_small, 16 * (GROUP + LAYERS))
            chain(v.tensor_copy(comp_part[0][:], comp[:]))
            chain(v.tensor_tensor(comp_rest[:], comp[:], comp_part[0][:], ALU.subtract))
            chain(v.tensor_copy(comp_part[1][:], comp_rest[:]))
            chain(v.tensor_tensor(comp_rest[:], comp_rest[:], comp_part[1][:], ALU.subtract))
            chain(v.tensor_copy(comp_part[2][:], comp_rest[:]), prepared)
            eng.wait_ge(att_spread, 1)
            chain(v.tensor_copy(att_all[:], psum[:, 7, 0:LAYERS * RELS * ATT]))
            eng.wait_ge(bucket_sum, 1)
            chain(v.tensor_scalar(bucket[:], order0.p_bucket, float(NB - 1), None, ALU.min))
            eng.wait_ge(carry_end, 1)
            chain(v.tensor_copy(source[:, 0:T0], psum[:, 2, 0:T0]))
            chain(v.tensor_copy(s_int, psum[:, 3, 0:T0]))
            chain(v.tensor_scalar(s_int_b, s_int, 5, None, ALU.arith_shift_right))
            chain(v.tensor_copy(place[:, 0:T0], s_int_b))
            chain(v.tensor_scalar(s_int, s_int, TYPES - 1, None, ALU.bitwise_and))
            chain(v.tensor_copy(kind[:, 0:T0], s_int))
            chain(v.tensor_copy(weight[:, 0:T0], psum[:, 4, 0:T0]))
            chain(v.tensor_tensor(weight[:, 0:T0], weight[:, 0:T0], psum[:, 5, 0:T0], ALU.add))
            chain(v.tensor_tensor(weight[:, 0:T0], weight[:, 0:T0], psum[:, 6, 0:T0], ALU.add), slots_made)

            def kinds(g):
                v.tensor_tensor(kind_hot[:], kind[:, ds(g * GROUP, GROUP)].unsqueeze(2).broadcast_to((P, GROUP, TYPES)),
                                count_t[:, 0:TYPES].unsqueeze(1).broadcast_to((P, GROUP, TYPES)),
                                ALU.is_equal).then_inc(hot_made, 1)

            def make_factors(g, ahead):
                cols = ds(g * GROUP, GROUP)
                v.tensor_tensor(place_hot[:], place[:, cols].unsqueeze(2).broadcast_to((P, GROUP, BN)),
                                count_t[:, 0:BN].unsqueeze(1).broadcast_to((P, GROUP, BN)),
                                ALU.is_equal).then_inc(factor_step, 1)
                eng.wait_ge(looked_up, g + 1)
                v.tensor_tensor(factor[:], psum[:, 5, 0:GROUP * BASES].rearrange("p (j b) -> p j b", j=GROUP),
                                weight[:, cols].unsqueeze(2).broadcast_to((P, GROUP, BASES)),
                                ALU.mult).then_inc(factor_step, 1)
                eng.wait_ge(factor_step, g * 2 + 2)
                return v.tensor_tensor(factors[:, ahead].rearrange("p j (n b) -> p j n b", b=BASES),
                                       factor[:].unsqueeze(2).broadcast_to((P, GROUP, BN, BASES)),
                                       place_hot[:].unsqueeze(3).broadcast_to((P, GROUP, BN, BASES)),
                                       ALU.mult).then_inc(factors_made, 1)

            kinds(0)
            eng.wait_ge(hot_turned, 1)
            kinds(1)
            make_factors(0, 0)
            eng.wait_ge(cleared, 4)
            with eng.Fori(0, T0 // DVE_TILES) as i, ExitStack() as held:
                regs = [held.enter_context(eng.register(f"bucket_{j}")) for j in range(DVE_TILES)]
                eng.load(regs, bucket[0:1, ds(i * DVE_TILES, DVE_TILES)])
                for h in range(DVE_TILES // GROUP):
                    g = i * (DVE_TILES // GROUP) + h
                    eng.wait_ge(hot_turned, g + 2)
                    kinds(g + 2)
                    for j in range(GROUP):
                        k = GROUP * h + j
                        b = eng.snap(regs[k], min_val=0, max_val=NB - 1)
                        into = sums[:, :, ds(b * P, P)]
                        added, done = (eng.snap(i * DVE_TILES + (k + n)) for n in (OPEN_BANKS, 1 + SLOTS))
                        eng.wait_ge(tile_done, done)
                        eng.wait_ge(tile_added, added)
                        v.tensor_tensor(into, into, psum[:, k % OPEN_BANKS, :].rearrange("p (c m) -> p c m", c=KC),
                                        ALU.add).then_inc(tile_added, 1)
                        if j == 0:
                            eng.wait_ge(tile_done, g * GROUP + SLOTS)
                            eng.wait_ge(factors_made, g + 1)
                            make_factors(g + 1, (h + 1) % 2)

            def mix_bases(chunks, first=0, end=ATT // WRING):
                for layer, c in chunks:
                    block_at = layer * KC + c - MIX_CHUNKS
                    if block_at and first == 0:
                        eng.wait_ge(st_mix, 16 * block_at)
                    if first == 0:
                        chain(v.memset(mix, 0.0))
                    with eng.Fori(first, end) as j:
                        for s in range(WRING):
                            eng.wait_ge(ld_basis[s], j * 16 + 16 * (block_at * (ATT // WRING) + 1))
                            for r in range(RELS):
                                eng.wait_ge(mixed, j * (WRING * RELS) + (block_at * ATT * RELS + RELS * s + r - 1 + 2 * WRING))
                                v.scalar_tensor_tensor(mix[:, r, :], basis_ring[:, s, :],
                                                       att_all[:, ds(j * WRING + ((layer * RELS + r) * ATT + s), 1)],
                                                       mix[:, r, :], ALU.mult, ALU.add).then_inc(mixed, 1)

            def add_layer0(half):
                for w in range(half * HALF, (half + 1) * HALF):
                    eng.wait_ge(layer0_done, w + 1)
                    chain(v.tensor_tensor(x_sb[0:rows(w), w, :], x_sb[0:rows(w), w, :], psum[0:rows(w), w % BANKS, :],
                                          ALU.add), x1_made)

            for half, chunks in enumerate((mix_left[:MIX_HALF], mix_left[MIX_HALF:])):
                mine = range(half * HALF, (half + 1) * HALF)
                if half == 0:
                    mix_bases(chunks[:-1])
                    eng.wait_ge(ld_x2, 16 * NW)
                    eng.wait_ge(ld_bias_first, 16)
                    for w in range(NW):
                        v.tensor_tensor(x_sb[0:rows(w), w, :], x_sb[0:rows(w), w, :], bias_all[0:rows(w), :],
                                        ALU.add).then_inc(bias_added, 1)
                    eng.wait_ge(bias_added, NW)
                    mix_bases(chunks[-1:], 0, MIX_CUT)
                    add_layer0(0)
                    mix_bases(chunks[-1:], MIX_CUT)
                else:
                    mix_bases(chunks)
                    add_layer0(1)
                norm_statistics(mine, rows)
                if half == 0:
                    norm_scales(mine, 2)
                    eng.wait_ge(ld_gates, 16 * LAYERS * RELS)
                    eng.wait_ge(normed, NW + HALF)
                    gate_sums(0, mine, h_n)

            chain(v.memset(row_of, 0), prepared)
            eng.wait_ge(ld_edges1, 48)
            chain(v.tensor_scalar(order1.int_a, g_src, 7, None, ALU.arith_shift_right))
            chain(v.tensor_copy(order1.key, order1.int_a))
            count_edges(order1)
            norm_scales(range(HALF, NW), 3)
            place_edges(order1, 1)
            chain(v.tensor_copy(g_row, g_dst))
            chain(v.tensor_scalar(order1.int_b, g_src, P - 1, None, ALU.bitwise_and))
            chain(v.tensor_scalar(g_place, order1.int_b, 1.0, 2.0, ALU.add, ALU.mult))
            chain(v.tensor_tensor(g_code, g_place, g_rel, ALU.add))
            eng.wait_ge(normed, 2 * NW)
            gate_sums(0, range(HALF, NW), h_n)
            slots_of_edges(order1, 1)
            eng.wait_ge(bucket_sum, 2)
            chain(v.tensor_scalar(window, order1.p_bucket, float(NW - 1), None, ALU.min), window_made)
            carry_edges(order1, sets1, [g_row, g_code], 1, PARTS1)
            eng.wait_ge(carry_end, 2)
            chain(v.tensor_copy(t_int, psum[:, 1, 0:T1]))
            chain(v.tensor_scalar(t_int_b, t_int, 1, None, ALU.arith_shift_right))
            chain(v.tensor_scalar(minus_local, t_int_b, -1.0, None, ALU.mult))
            chain(v.tensor_scalar(t_int, t_int, 1, None, ALU.bitwise_and))
            chain(v.tensor_scalar(t_f, t_int, float(N), None, ALU.mult))
            chain(v.tensor_tensor(row_of[:, 0:T1], t_f, psum[:, 0, 0:T1], ALU.add), slots1_made)

            for layer in range(LAYERS):
                if layer:
                    eng.wait_ge(tile1_added, layer * T1 + OPEN_BANKS)
                    gate_sums(layer, range(NW), acc)
                sums1, sums1_w = (region_x, x_sb) if layer else (acc_flat, acc)
                if layer == 0:
                    eng.wait_ge(ld_acc, 16 * NW)
                else:
                    eng.wait_ge(ld_bias, 16)
                    for w in range(NW):
                        v.tensor_tensor(x_sb[0:rows(w), w, :], x_sb[0:rows(w), w, :], bias_all[0:rows(w), :],
                                        ALU.add).then_inc(bias_added, 1)
                    eng.wait_ge(bias_added, 2 * NW)

                def add_tile(i, k, reg, roots):
                    at = eng.snap(reg, min_val=0, max_val=NW - 1)
                    into = sums1[:, ds(at * D, D)]
                    eng.wait_ge(tile1_done, i * PE_TILES + (layer * T1 + k + 1 + SLOTS1))
                    eng.wait_ge(tile1_added, i * PE_TILES + (layer * T1 + k + OPEN_BANKS))
                    if roots:
                        eng.wait_ge(root_in, layer * NW + roots)
                    v.tensor_tensor(into, into, psum[:, 4 + k % OPEN_BANKS, :], ALU.add).then_inc(tile1_added, 1)

                def add_root(w):
                    eng.wait_ge(root_sum, layer * NW + w + 1)
                    v.tensor_tensor(sums1_w[0:rows(w), w, :], sums1_w[0:rows(w), w, :], psum[0:rows(w), 2 + w % 2, :],
                                    ALU.add).then_inc(root_in, 1)

                for w in range(ROOTS_FIRST[layer]):
                    add_root(w)
                with ExitStack() as held:
                    regs = [held.enter_context(eng.register(f"window_{layer}_{j}")) for j in range(PE_TILES)]
                    added = ROOTS_FIRST[layer]
                    for i in range(FETCHES1 // PE_TILES):
                        eng.load(regs, window[0:1, i * PE_TILES:(i + 1) * PE_TILES])
                        for k in range(PE_TILES):
                            add_tile(i, k, regs[k], added)
                            n = i * PE_TILES + k
                            w = n // ROOT_EVERY - 1
                            if n % ROOT_EVERY == ROOT_EVERY - 1 and ROOTS_FIRST[layer] <= w < NW:
                                eng.wait_ge(tile1_added, layer * T1 + n + 1 + OPEN_BANKS)
                                add_root(w)
                                added = w + 1
                    with eng.Fori(FETCHES1 // PE_TILES, T1 // PE_TILES) as i:
                        eng.load(regs, window[0:1, ds(i * PE_TILES, PE_TILES)])
                        for k in range(PE_TILES):
                            add_tile(i, k, regs[k], 0)

        @block.tensor
        def _(pe):
            mm = nc.tensor.matmul
            pe.sem_inc(tile_done, SLOTS)
            pe.sem_inc(tile1_done, SLOTS1)
            pe.sem_inc(base_used, 2)
            pe.sem_inc(mix_read, MRING)
            for k in range(2):
                pe.sem_inc(carried[k], 1)

            def count_totals(o, n):
                pe.wait_ge(counted, n + 1)
                mm(o.p_before, before_b[0:EP, 0:EP], o.own, start=True, stop=True)
                mm(o.p_total, ones_b[0:EP, 0:EP], o.own, start=True, stop=True)
                mm(o.p_down, o.own, ones_b[0:EP, 0:1], start=True, stop=True).then_inc(total, 1)

            def count_tiles(o, n):
                pe.wait_ge(tiles_down, n + 1)
                mm(o.p_end, before_b[0:o.nb, 0:o.nb], o.col_nt, start=True, stop=False)
                mm(o.p_end, ident_b[0:o.nb, 0:o.nb], o.col_nt, start=False, stop=True).then_inc(ends_down, 1)

            def sum_buckets(o, n):
                pe.wait_ge(past_made, n + 1)
                mm(o.p_bucket, ones_b[0:o.nb, 0:1], o.past, start=True, stop=True).then_inc(bucket_sum, 1)

            def sum_slots(o, n):
                pe.wait_ge(split, n + 1)
                for out_, table in ((o.p_low, o.count), (o.p_high, o.base)):
                    for k in range(o.nb):
                        last = mm(out_, ident_b[0:EP, 0:EP], table[:, k * ET:(k + 1) * ET], start=(k == 0), stop=(k == o.nb - 1))
                last.then_inc(slot_sum, 1)

            def carry_open(banks, o, stop=False):
                for b in banks:
                    last = mm(psum[:, b, 0:o.tiles], zeros_b[0:EP, :], count_t[0:EP, 0:o.tiles], start=not stop, stop=stop,
                              skip_group_check=True)
                return last

            def carry_chunk(sets, fields, banks, o, k, ready):
                pe.wait_ge(carry_made[k], ready)
                if o is order0:
                    pe.wait_ge(last_made[k], ready)
                _, row_parts, tile_hot = sets[k]
                for t in range(TC):
                    for part, field, b in zip(row_parts, fields, banks):
                        last = mm(psum[:, b, 0:o.tiles], part_of(part, field)[:, :, t], tile_hot[:, :, t],
                                  start=False, stop=False, skip_group_check=True)
                last.then_inc(carried[k], 1)

            def mix_steps(g, parts):
                for part in parts:
                    n = g * MIX_PARTS + part
                    pe.wait_ge(ld_mix[n % MRING], 64 * (n // MRING + 1))
                    if part == 0 and g:
                        pe.wait_ge(mix_copied, g)
                    for t in range(MIX_LOAD):
                        s = part * MIX_LOAD + t
                        last = mm(psum[:, 7, :], mix_att[:, MIX_STEPS - 1 - s:MIX_STEPS - 1 - s + P],
                                  mix_load[:, n % MRING, t, :], start=(s == 0), stop=(s == MIX_STEPS - 1))
                    last.then_inc(mix_read, 1)

            pe.wait_ge(ld_att, 16 * RELS * 4)
            mix_steps(0, range(MIX_PARTS))
            mix_steps(1, range(MIX_PARTS))
            pe.wait_ge(prepared, 1)
            count_totals(order0, 0)
            count_tiles(order0, 0)
            for g in range(2, MIX_EARLY):
                mix_steps(g, range(MIX_PARTS))
            sum_slots(order0, 0)
            sum_buckets(order0, 0)
            for g in range(MIX_EARLY, MIX_GROUPS):
                mix_steps(g, range(MIX_PARTS))
            fields0 = [f_source, f_code, *f_weight]
            banks0 = range(2, 2 + PARTS)
            carry_open(banks0, order0)
            with pe.Fori(0, CHUNKS // 2) as i:
                for k in range(2):
                    carry_chunk(sets0, fields0, banks0, order0, k, i + 1)
            carry_open(banks0, order0, stop=True).then_inc(carry_end, 1)
            pe.wait_ge(ld_small, 16 * (GROUP + LAYERS))
            pe.wait_ge(mix_copied, MIX_GROUPS)
            mm(psum[:, 7, 0:LAYERS * RELS * ATT], ones_row[:], att_row[:], start=True, stop=True).then_inc(att_spread, 1)

            def turn_kinds():
                nc.tensor.transpose(turn_bank, kind_hot[:].rearrange("p j k -> p (j k)"), ident_b[:]).then_inc(hot_turned, 1)

            def look_up():
                for k in range(3):
                    last = mm(psum[:, 5, 0:GROUP * BASES], kind_hot_t[:], comp_part[k][:], start=(k == 0), stop=(k == 2))
                last.then_inc(looked_up, 1)

            pe.wait_ge(slots_made, 1)
            pe.wait_ge(prepared, 2)
            pe.wait_ge(hot_made, 1)
            turn_kinds()
            pe.wait_ge(hot_made, 2)
            pe.wait_ge(hot_copied, 1)
            turn_kinds()
            look_up()
            with pe.Fori(0, T0 // PE_TILES) as i:
                for h in range(2):
                    g = i * 2 + h
                    pe.wait_ge(factors_made, g + 1)
                    for j in range(GROUP):
                        k = GROUP * h + j
                        pe.wait_ge(fetched[k], i * 16 + 16)
                        pe.wait_ge(tile_added, i * PE_TILES + (k + 1))
                        for c in range(KC):
                            last = mm(psum[:, k % OPEN_BANKS, c * P:(c + 1) * P], ring0[:, k, c * P:(c + 1) * P],
                                      factors[:, h, j, :], start=True, stop=True)
                        last.then_inc(tile_done, 1)
                        if j == 0:
                            pe.wait_ge(hot_copied, g + 2)
                            look_up()
                        elif j == 1:
                            pe.wait_ge(hot_made, g + 3)
                            turn_kinds()

            pe.wait_ge(tile_added, T0 + OPEN_BANKS)
            pe.wait_ge(hot_copied, T0 // GROUP + 2)
            pe.wait_ge(factors_made, T0 // GROUP + 1)
            for half in range(2):
                mine = range(half * HALF, (half + 1) * HALF)
                per = P // BN
                for w in mine:
                    m = min(P, (NB - per * w) * BN)
                    if w >= BANKS:
                        pe.wait_ge(x1_made, w - BANKS + 1)
                for b in range(BASES):
                    for c in range(KC):
                        chunk = (half * BASES + b) * KC + c
                        pe.wait_ge(ld_base[chunk % 2], 16 * (chunk // 2 + 1))
                        end = b == BASES - 1 and c == KC - 1
                        for w in mine:
                            m = min(P, (NB - per * w) * BN)
                            last = mm(psum[0:m, w % BANKS, :], sums[:, c, per * w * P + b:(per * w + m // BN) * P:BASES],
                                      base_ring[:, chunk % 2, :], start=(b == 0 and c == 0), stop=end)
                            if end:
                                last.then_inc(layer0_done, 1)
                            elif half and chunk == BASES * KC and w == HALF:
                                last.then_inc(base_used, 1)
                        if not end:
                            last.then_inc(base_used, 1)

            for layer in range(LAYERS):
                rows_in = h_n if layer == 0 else acc
                if layer:
                    pe.wait_ge(tile1_added, layer * T1 + OPEN_BANKS)
                    pe.wait_ge(root_in, layer * NW)
                def multiply_root(w):
                    if w >= 2:
                        pe.wait_ge(root_in, layer * NW + w - 1)
                    for c in range(KC):
                        last = mm(psum[0:rows(w), 2 + w % 2, :], h_t[:, c, w * P:w * P + rows(w)], root_sb[:, c, :],
                                  start=(c == 0), stop=(c == KC - 1))
                    last.then_inc(root_sum, 1)

                chunks = iter(range(CHUNKS))

                def carry_one():
                    n = next(chunks, None)
                    if n == 0:
                        pe.wait_ge(window_made, 1)
                        carry_open(range(2), order1)
                    if n is not None:
                        carry_chunk(sets1, [g_row, g_code], range(2), order1, n % 2, CHUNKS // 2 + n // 2 + 1)
                    if n == CHUNKS - 1:
                        carry_open(range(2), order1, stop=True).then_inc(carry_end, 1)

                for w in range(NW + 1):
                    if w < NW:
                        if layer == 0:
                            pe.wait_ge(normed, NW + w + 1)
                        if w >= 2:
                            pe.wait_ge(turned_sb, layer * NW + w - 1)
                        for c in range(KC):
                            last = nc.tensor.transpose(psum[:, 2 + w % 2, c * P:c * P + rows(w)],
                                                       rows_in[0:rows(w), w, c * P:(c + 1) * P], ident[0:rows(w), 0:rows(w)])
                        last.then_inc(turned, 1)
                    if w == 0:
                        pe.wait_ge(ld_w[layer], 16 * (RELS + 1))
                        continue
                    at = w - 1
                    pe.wait_ge(turned_sb, layer * NW + at + 1)
                    for r in range(RELS):
                        if layer == 0 and at > CARRY_FROM:
                            carry_one()
                            carry_one()
                        n = (layer * NW + at) * RELS + r
                        if n < BANKS - 4:
                            pe.wait_ge(x1_made, HALF + n)
                        elif at * RELS + r >= 4:
                            pe.wait_ge(product_sb, n - 3)
                        for c in range(KC):
                            last = mm(psum[0:rows(at), 4 + n % 4, :], h_t[:, c, at * P:at * P + rows(at)], w_sb[:, r, c, :],
                                      start=(c == 0), stop=(c == KC - 1))
                        last.then_inc(product, 1)
                    if layer:
                        continue
                    if at in ROOTS_AT:
                        multiply_root(ROOTS_AT.index(at))
                    if at == 1:
                        pe.wait_ge(x1_made, NW)
                        count_totals(order1, 1)
                    elif at == 2:
                        count_tiles(order1, 1)
                    elif at == 3:
                        sum_slots(order1, 1)
                        sum_buckets(order1, 1)

                if layer == 0:
                    for _ in range(CHUNKS):
                        carry_one()

                def multiply_tile(i, k):
                    pe.wait_ge(slot_hot_made, i * FETCHES1 + (layer * T1 + k + 1))
                    pe.wait_ge(fetched1[k % SLOTS1],
                               i * (16 * FETCHES1 // SLOTS1) + 16 * (layer * T1 // SLOTS1 + k // SLOTS1 + 1))
                    pe.wait_ge(tile1_added, i * FETCHES1 + (layer * T1 + k + 1))
                    mm(psum[:, 4 + k % OPEN_BANKS, :], slot_hot[:, k % PE_TILES, :], ring1[k % SLOTS1],
                       start=True, stop=True).then_inc(tile1_done, 1)

                pe.wait_ge(turned_sb, (layer + 1) * NW)
                pe.wait_ge(slots1_made, 1)
                pe.wait_ge(product_sb, (layer + 1) * NW * RELS)
                ahead = ROOTS_FIRST[layer]
                for w in range(0 if layer else len(ROOTS_AT), ahead):
                    multiply_root(w)
                for k in range(FETCHES1):
                    multiply_tile(0, k)
                    if k % ROOT_EVERY == ROOT_EVERY - 3 and ahead <= k // ROOT_EVERY < NW:
                        multiply_root(k // ROOT_EVERY)
                with pe.Fori(1, T1 // FETCHES1) as i:
                    for k in range(FETCHES1):
                        multiply_tile(i, k)


_INS = ["x", "src", "dst", "edge_type_2", "edge_type_32", "edge_weight1", "L0_gnn_bases", "L0_gnn_w_comp",
        "L0_gnn_h_bias", "L1_gnn_basis1", "L1_gnn_att1", "L1_gnn_gate_w1", "L1_gnn_root1", "L1_gnn_bias1",
        "L1_gnn_basis2", "L1_gnn_att2", "L1_gnn_gate_w2", "L1_gnn_root2", "L1_gnn_bias2"]


def build(nc, a, out):
    gnn(nc, a["x"], a["src"], a["dst"], a["edge_type_2"], a["edge_type_32"], a["edge_weight1"], a["L0_gnn_bases"],
        a["L0_gnn_w_comp"], a["L0_gnn_h_bias"],
        *([a[f"L1_gnn_{name}{n}"] for n in (1, 2)] for name in ("basis", "att", "gate_w", "root", "bias")), out)


def kernel(**inputs):
    import numpy as np
    import concourse.bacc as bacc
    from concourse.bass_utils import run_bass_kernel_spmd

    nc = bacc.Bacc("TRN2", target_bir_lowering=False, num_devices=1)
    arrays = {f"in_{n}": np.ascontiguousarray(inputs[n]) for n in _INS}
    args = {n: nc.dram_tensor(f"in_{n}", arrays[f"in_{n}"].shape, mybir.dt.from_np(arrays[f"in_{n}"].dtype),
                              kind="ExternalInput").ap() for n in _INS}
    out = nc.dram_tensor("out", (N, D), F32, kind="ExternalOutput").ap()
    build(nc, args, out)
    return run_bass_kernel_spmd(nc, [arrays], core_ids=[0]).results[0]["out"]
```
